# Optimizing a Trainium2 kernel written in Bass

```python
import numpy as np
import jax
import jax.numpy as jnp

def _softmax(x, axis=-1):
    return jax.nn.softmax(x, axis=axis)

def _gelu(x):
    return jax.nn.gelu(x, approximate=True)

def _silu(x):
    return jax.nn.silu(x)

def _sigmoid(x):
    return jax.nn.sigmoid(x)

def _layernorm(x, axis=-1, eps=1e-05):
    m = jnp.mean(x, axis=axis, keepdims=True)
    v = jnp.var(x, axis=axis, keepdims=True)
    return (x - m) / jnp.sqrt(v + eps)

def _scatter_add(tgt, idx, src, axis=0):
    return tgt.at[idx].add(src)

def _segment_sum(src, seg, n):
    return jax.ops.segment_sum(src, seg, n)
kernel_name = 'mk_decoder_postln_d1_seqx_r8_77d78c'

def setup_inputs(seed: int=0):
    np.random.seed(seed)
    _w = jnp.asarray

    def _rec_inputs():
        import jax
        import jax.numpy as jnp
        _rk = jax.random.key(seed)
        x = -9.806e-05 + 1 * jax.random.normal(jax.random.fold_in(_rk, 1), (64, 128, 128), jnp.float32)
        _lenS = 128 - jax.random.randint(jax.random.fold_in(_rk, 7), (64,), 0, max(1, 128 // 4) + 1, jnp.int32)
        _lenS2 = 77 - jax.random.randint(jax.random.fold_in(_rk, 8), (64,), 0, max(1, 77 // 4) + 1, jnp.int32)
        _ctx_1024P = jax.random.normal(jax.random.fold_in(_rk, 11), (64, 16, 128), jnp.float32)
        _ctx_1024c = jax.random.dirichlet(jax.random.fold_in(_rk, 511), 0.3 * jnp.ones((16,), jnp.float32), (64, 77))
        _ctx_1024t = jnp.einsum('bsk,bkd->bsd', _ctx_1024c, _ctx_1024P)
        _ctx_1024t = _ctx_1024t * jax.lax.rsqrt(jnp.mean(jnp.square(_ctx_1024t)) + 1e-12) * 0.953939
        ctx_1024 = -1.52775e-05 + 0.999936 * (_ctx_1024t + 0.3 * jax.random.normal(jax.random.fold_in(_rk, 611), (64, 77, 128), jnp.float32))
        return (x, ctx_1024)
    x, ctx_1024 = _rec_inputs()

    def _L0_attn_setup():
        import jax, jax.numpy as jnp
        import numpy as np
        D_CONV = 4
        DT_RANK = 64
        D_STATE = 16

        def silu(v):
            return v * jax.nn.sigmoid(v)
        key = jax.random.key(seed)
        ks = jax.random.split(key, 10)
        B, L, d_model, d_inner = (2, 256, 128, 256)

        def nrm(k, shape, scale):
            return jax.random.normal(k, shape, dtype=jnp.float32) * scale
        A = jnp.tile(jnp.arange(1, D_STATE + 1, dtype=jnp.float32), (d_inner, 1))
        return {'x': nrm(ks[0], (B, L, d_model), 1.0), 'W_in': nrm(ks[1], (d_model, 2 * d_inner), d_model ** (-0.5)), 'conv_w': nrm(ks[2], (d_inner, D_CONV), D_CONV ** (-0.5)), 'conv_b': nrm(ks[3], (d_inner,), 0.02), 'W_x': nrm(ks[4], (d_inner, DT_RANK + 2 * D_STATE), d_inner ** (-0.5)), 'W_dt': nrm(ks[5], (DT_RANK, d_inner), DT_RANK ** (-0.5)), 'b_dt': nrm(ks[6], (d_inner,), 0.02), 'A_log': jnp.log(A), 'D': jnp.ones((d_inner,), dtype=jnp.float32), 'W_out': nrm(ks[7], (d_inner, d_model), d_inner ** (-0.5))}
    _L0_attn_all = _L0_attn_setup()
    _L0_attn_in = {k: v for k, v in _L0_attn_all.items() if k in ('W_in', 'conv_w', 'conv_b', 'W_x', 'W_dt', 'b_dt', 'A_log', 'D', 'W_out')}
    del _L0_attn_all

    def _L0_xattn_setup():
        import jax, jax.numpy as jnp
        import numpy as np
        D = 128
        NUM_ITERS = 3
        EPS = 1e-06
        SCALE = D ** (-0.5)

        def rmsnorm(x, w, eps=EPS):
            return x * jax.lax.rsqrt(jnp.mean(x * x, axis=-1, keepdims=True) + eps) * w

        def gru_cell(x, h, wih, whh, bih, bhh):
            gx = x @ wih.T + bih
            gh = h @ whh.T + bhh
            xr, xz, xn = jnp.split(gx, 3, axis=-1)
            hr, hz, hn = jnp.split(gh, 3, axis=-1)
            r = jax.nn.sigmoid(xr + hr)
            z = jax.nn.sigmoid(xz + hz)
            n = jnp.tanh(xn + r * hn)
            return (1.0 - z) * n + z * h
        key = jax.random.key(seed)
        ks = jax.random.split(key, 8)
        B, K, M, d = (8, 64, 512, D)
        w_std = d ** (-0.5)
        return {'slots': jax.random.normal(ks[0], (B, K, d), jnp.float32), 'P': jax.random.normal(ks[1], (B, M, d), jnp.float32), 'Wq': jax.random.normal(ks[2], (d, d), jnp.float32) * w_std, 'Wk': jax.random.normal(ks[3], (d, d), jnp.float32) * w_std, 'Wv': jax.random.normal(ks[4], (d, d), jnp.float32) * w_std, 'gru_wih': jax.random.normal(ks[5], (3 * d, d), jnp.float32) * w_std, 'gru_whh': jax.random.normal(ks[6], (3 * d, d), jnp.float32) * w_std, 'gru_bih': jnp.zeros((3 * d,), jnp.float32), 'gru_bhh': jnp.zeros((3 * d,), jnp.float32), 'slot_norm_w': jnp.ones((d,), jnp.float32), 'input_norm_w': jnp.ones((d,), jnp.float32)}
    _L0_xattn_all = _L0_xattn_setup()
    _L0_xattn_in = {k: v for k, v in _L0_xattn_all.items() if k in ('Wq', 'Wk', 'Wv', 'gru_wih', 'gru_whh', 'gru_bih', 'gru_bhh', 'slot_norm_w', 'input_norm_w')}
    del _L0_xattn_all

    def _L0_ffn_setup():
        import jax, jax.numpy as jnp
        import numpy as np
        B, S, H, FFN, E = (2, 256, 128, 512, 8)
        key = jax.random.key(seed)
        k0, k1, k2, k3 = jax.random.split(key, 4)
        return {'hidden_states': jax.random.normal(k0, (B, S, H), dtype=jnp.float32), 'Wr': jax.random.normal(k1, (H, E), dtype=jnp.float32) * 0.02, 'br': jnp.zeros((E,), dtype=jnp.float32), 'W1': jax.random.normal(k2, (E, H, FFN), dtype=jnp.float32) * 0.02, 'W2': jax.random.normal(k3, (E, FFN, H), dtype=jnp.float32) * 0.02}
    _L0_ffn_all = _L0_ffn_setup()
    _L0_ffn_in = {k: v for k, v in _L0_ffn_all.items() if k in ('Wr', 'br', 'W1', 'W2')}
    del _L0_ffn_all
    return {'x': x, 'ctx_1024': ctx_1024, 'L0_attn_W_in': _L0_attn_in['W_in'], 'L0_attn_conv_w': _L0_attn_in['conv_w'], 'L0_attn_conv_b': _L0_attn_in['conv_b'], 'L0_attn_W_x': _L0_attn_in['W_x'], 'L0_attn_W_dt': _L0_attn_in['W_dt'], 'L0_attn_b_dt': _L0_attn_in['b_dt'], 'L0_attn_A_log': _L0_attn_in['A_log'], 'L0_attn_D': _L0_attn_in['D'], 'L0_attn_W_out': _L0_attn_in['W_out'], 'L0_xattn_Wq': _L0_xattn_in['Wq'], 'L0_xattn_Wk': _L0_xattn_in['Wk'], 'L0_xattn_Wv': _L0_xattn_in['Wv'], 'L0_xattn_gru_wih': _L0_xattn_in['gru_wih'], 'L0_xattn_gru_whh': _L0_xattn_in['gru_whh'], 'L0_xattn_gru_bih': _L0_xattn_in['gru_bih'], 'L0_xattn_gru_bhh': _L0_xattn_in['gru_bhh'], 'L0_xattn_slot_norm_w': _L0_xattn_in['slot_norm_w'], 'L0_xattn_input_norm_w': _L0_xattn_in['input_norm_w'], 'L0_ffn_Wr': _L0_ffn_in['Wr'], 'L0_ffn_br': _L0_ffn_in['br'], 'L0_ffn_W1': _L0_ffn_in['W1'], 'L0_ffn_W2': _L0_ffn_in['W2']}

def reference(x, ctx_1024, L0_attn_W_in, L0_attn_conv_w, L0_attn_conv_b, L0_attn_W_x, L0_attn_W_dt, L0_attn_b_dt, L0_attn_A_log, L0_attn_D, L0_attn_W_out, L0_xattn_Wq, L0_xattn_Wk, L0_xattn_Wv, L0_xattn_gru_wih, L0_xattn_gru_whh, L0_xattn_gru_bih, L0_xattn_gru_bhh, L0_xattn_slot_norm_w, L0_xattn_input_norm_w, L0_ffn_Wr, L0_ffn_br, L0_ffn_W1, L0_ffn_W2):
    import jax
    import jax.numpy as jnp

    def _L0_attn_ref(x, W_in, conv_w, conv_b, W_x, W_dt, b_dt, A_log, D, W_out):
        import jax, jax.numpy as jnp
        import numpy as np
        D_CONV = 4
        DT_RANK = 64
        D_STATE = 16

        def silu(v):
            return v * jax.nn.sigmoid(v)
        B, L, _ = x.shape
        d_inner = W_dt.shape[1]
        xz = x @ W_in
        xb, z = jnp.split(xz, 2, axis=-1)
        xp = jnp.pad(xb, ((0, 0), (D_CONV - 1, 0), (0, 0)))
        xc = sum((xp[:, k:k + L, :] * conv_w[:, k] for k in range(D_CONV))) + conv_b
        xb = silu(xc)
        x_dbl = xb @ W_x
        dt_low, Bm, Cm = jnp.split(x_dbl, [DT_RANK, DT_RANK + D_STATE], axis=-1)
        dt = jax.nn.softplus(dt_low @ W_dt + b_dt)
        A = -jnp.exp(A_log)

        def step(h, inp):
            dt_t, B_t, C_t, x_t = inp
            dA = jnp.exp(A * dt_t[..., None])
            h = h * dA + (x_t * dt_t)[..., None] * B_t[:, None, :]
            y = jnp.einsum('bdn,bn->bd', h, C_t)
            return (h, y)
        xs = (dt.swapaxes(0, 1), Bm.swapaxes(0, 1), Cm.swapaxes(0, 1), xb.swapaxes(0, 1))
        h0 = jnp.zeros((B, d_inner, D_STATE), dtype=x.dtype)
        _, ys = jax.lax.scan(step, h0, xs)
        y = ys.swapaxes(0, 1) + xb * D
        out = y * silu(z)
        return out @ W_out

    def _L0_xattn_ref(slots, P, Wq, Wk, Wv, gru_wih, gru_whh, gru_bih, gru_bhh, slot_norm_w, input_norm_w):
        import jax, jax.numpy as jnp
        import numpy as np
        D = 128
        NUM_ITERS = 3
        EPS = 1e-06
        SCALE = D ** (-0.5)

        def rmsnorm(x, w, eps=EPS):
            return x * jax.lax.rsqrt(jnp.mean(x * x, axis=-1, keepdims=True) + eps) * w

        def gru_cell(x, h, wih, whh, bih, bhh):
            gx = x @ wih.T + bih
            gh = h @ whh.T + bhh
            xr, xz, xn = jnp.split(gx, 3, axis=-1)
            hr, hz, hn = jnp.split(gh, 3, axis=-1)
            r = jax.nn.sigmoid(xr + hr)
            z = jax.nn.sigmoid(xz + hz)
            n = jnp.tanh(xn + r * hn)
            return (1.0 - z) * n + z * h
        Pn = rmsnorm(P, input_norm_w)
        k_proj = Pn @ Wk.T
        v_proj = Pn @ Wv.T
        for _ in range(NUM_ITERS):
            sn = rmsnorm(slots, slot_norm_w)
            q_proj = sn @ Wq.T
            scores = jnp.einsum('bkd,bmd->bkm', q_proj, k_proj) * SCALE
            attn = jax.nn.softmax(scores, axis=-2)
            attn = attn / (jnp.sum(attn, axis=-1, keepdims=True) + EPS)
            updates = jnp.einsum('bkm,bmd->bkd', attn, v_proj)
            slots = gru_cell(updates, slots, gru_wih, gru_whh, gru_bih, gru_bhh)
        return slots

    def _L0_ffn_ref(hidden_states, Wr, br, W1, W2):
        import jax, jax.numpy as jnp
        import numpy as np
        B, S, H, FFN, E = (2, 256, 128, 512, 8)
        b, s, h = hidden_states.shape
        x = hidden_states.reshape(-1, h)
        route = jax.nn.sigmoid(x @ Wr + br)
        max_prob = jnp.max(route, axis=1, keepdims=True)
        max_ind = jnp.argmax(route, axis=1)
        out = jnp.zeros_like(x)
        n_experts = Wr.shape[1]
        for e in range(n_experts):
            mask = (max_ind == e)[:, None].astype(x.dtype)
            y = jax.nn.gelu(x @ W1[e], approximate=False) @ W2[e]
            out = out + mask * y
        out = out * max_prob
        return out.reshape(b, s, h)
    x = _layernorm(x + _L0_attn_ref(x, L0_attn_W_in, L0_attn_conv_w, L0_attn_conv_b, L0_attn_W_x, L0_attn_W_dt, L0_attn_b_dt, L0_attn_A_log, L0_attn_D, L0_attn_W_out), axis=-1)
    x = _layernorm(x + _L0_xattn_ref(x, ctx_1024, L0_xattn_Wq, L0_xattn_Wk, L0_xattn_Wv, L0_xattn_gru_wih, L0_xattn_gru_whh, L0_xattn_gru_bih, L0_xattn_gru_bhh, L0_xattn_slot_norm_w, L0_xattn_input_norm_w), axis=-1)
    x = _layernorm(x + _L0_ffn_ref(x, L0_ffn_Wr, L0_ffn_br, L0_ffn_W1, L0_ffn_W2), axis=-1)
    return x

_drawn_inputs = setup_inputs


def setup_inputs(seed=0):
    import zlib

    import numpy as np

    out = dict(_drawn_inputs(seed))
    spreads = {'L0_attn_D': (1.0, 0.2),
     'L0_xattn_gru_bih': (0.0, 0.1),
     'L0_xattn_gru_bhh': (0.0, 0.1),
     'L0_xattn_slot_norm_w': (1.0, 0.6),
     'L0_xattn_input_norm_w': (1.0, 0.2),
     'L0_ffn_br': (0.0, 0.273)}
    factors = {'L0_attn_conv_b': 3.873, 'L0_attn_b_dt': 8.0}
    for name, (base, spread) in spreads.items():
        noise = np.random.default_rng([zlib.crc32(name.encode()), seed]).standard_normal(out[name].shape)
        drawn = base * np.exp(spread * noise) if base else spread * noise
        out[name] = jnp.asarray(drawn.astype(out[name].dtype))
    for name, factor in factors.items():
        out[name] = (out[name] * factor).astype(out[name].dtype)
    return out
```

```python
from contextlib import ExitStack

import concourse.bass as bass
from concourse import mybir

ALU = mybir.AluOpType
ACT = mybir.ActivationFunctionType
F32 = mybir.dt.float32
BF16 = mybir.dt.bfloat16
I32 = mybir.dt.int32
AX_X = mybir.AxisListType.X

P = 128
GB = 4
T = GB * P
HUGE = 1.0e30
LN_EPS = 1e-5
RMS_EPS = 1e-6


def after(count_per_group, k, g):
    return g * count_per_group + (k + 1)


def need(eng, sem, value):
    if isinstance(value, int) and value <= 0:
        return
    eng.wait_ge(sem, value)


def hold(eng, sem, value, passed):
    eng.wait_ge(sem, value)
    eng.sem_inc(passed, 1)


def places(nc, stage):
    def sb(name, shape, dt=F32):
        return stage.enter_context(nc.sbuf_tensor(name, shape, dt))

    def psum(name, shape, dt=F32):
        return stage.enter_context(nc.psum_tensor(name, shape, dt))

    def sem(name):
        return stage.enter_context(nc.semaphore(name))

    return sb, psum, sem


def build_program(nc, t, out):
    x, ctx_in = t["x"], t["ctx_1024"]
    B, L, D = x.shape
    DI = t["L0_attn_D"].shape[0]
    NS = t["L0_attn_A_log"].shape[1]
    R = t["L0_attn_W_dt"].shape[0]
    C = DI // P
    NG = B // GB
    NT = B * L
    assert L == P and D == P and C == 2 and R + 2 * NS == 96 and T == 512 and NG % 2 == 0

    with ExitStack() as stack:
        ident = stack.enter_context(nc.sbuf_tensor("ident", [P, P], F32))
        x2 = stack.enter_context(nc.sbuf_tensor("x2", [P, B, D], F32))
        with ExitStack() as first_two:
            x1T = first_two.enter_context(nc.sbuf_tensor("x1T", [P, NT], F32))
            with ExitStack() as stage:
                mamba_stage(nc, t, *places(nc, stage), x1T, ident, NG, NS, C, R)
            with ExitStack() as stage:
                slot_stage(nc, t, *places(nc, stage), x1T, x2, ident, NG)
        with ExitStack() as stage:
            expert_stage(nc, t, *places(nc, stage), x2, ident, out)


def mamba_stage(nc, t, sb, psum, sem, x1T, ident, NG, NS, C, R):
    U = NS * C
    w_in = sb("w_in", [P, 4 * P])
    conv_w = sb("conv_w", [P, C, 4])
    conv_b = sb("conv_b", [P, C])
    w_dtlow = sb("w_dtlow", [P, C, R])
    w_bc3 = sb("w_bc3", [P, C, 3, 2 * NS])
    w_dt = sb("w_dt", [R, C * P])
    b_dt = sb("b_dt", [P, C])
    a_neg = sb("a_neg", [P, C, NS])
    d_half = sb("d_half", [P, C])
    w_out = sb("w_out", [P, C, P])
    pick = sb("pick", [96, 2 * NS, P], BF16)
    minus_half = sb("minus_half", [P, GB])
    x_tok = sb("x_tok", [P, GB, P])
    x_res = sb("x_res", [P, GB, P])
    xT = sb("xT", [P, T])
    xb_pad = sb("xb_pad", [P, C, GB, P + 3])
    xc = sb("xc", [P, C, T])
    th = sb("th", [P, C, T])
    thz = sb("thz", [P, C, T])
    xb2 = sb("xb2", [P, 2, C, T])
    sz2 = sb("sz2", [P, 2, C, T])
    dt_low = sb("dt_low", [R, T])
    bc_split = sb("bc_split", [96, 2, T], BF16)
    bc_rest = sb("bc_rest", [96, T])
    bc_mid = sb("bc_mid", [96, T], BF16)
    sp_abs = sb("sp_abs", [P, C, T])
    sp_relu = sb("sp_relu", [P, C, T])
    dt = sb("dt", [P, 2, C, T])
    dtx = sb("dtx", [P, 2, C, T])
    inp = sb("inp", [P, 4, T])
    state = sb("state", [P, 4, T])
    c_bc = sb("c_bc", [P, 2, T])
    hc = sb("hc", [P, 4, T])
    yd = sb("yd", [P, C, T])
    yz = sb("yz", [P, C, T])
    res = sb("res", [P, GB, P])
    stats = sb("stats", [P, GB, 6])
    mv = sb("mv", [P, GB, 2])
    veps = sb("veps", [P, GB])
    rstd = sb("rstd", [P, GB])
    ps_misc = psum("ps_misc", [P, T])
    ps_da = [psum(f"ps_da{i}", [P, T]) for i in range(2)]
    ps_b = [psum(f"ps_b{i}", [P, T]) for i in range(2)]
    ps_c = psum("ps_c", [P, T])
    ps_y = [psum(f"ps_y{c}", [P, T]) for c in range(C)]

    w_loaded = sem("w_loaded")
    consts_pool = sem("consts_pool")
    w_scaled = sem("w_scaled")
    a_ready = sem("a_ready")
    x_loaded = sem("x_loaded")
    res_loaded = sem("res_loaded")
    misc_full = sem("misc_full")
    act_pre = sem("act_pre")
    dve_pre = sem("dve_pre")
    pool_pre = sem("pool_pre")
    da_ready = sem("da_ready")
    b_ready = sem("b_ready")
    c_full = sem("c_full")
    c_ready = sem("c_ready")
    inp_ready = sem("inp_ready")
    state_ready = sem("state_ready")
    hc_ready = sem("hc_ready")
    y_added = sem("y_added")
    y_taken = sem("y_taken")
    yz_ready = sem("yz_ready")
    res_ready = sem("res_ready")
    ln_step = sem("ln_step")
    rstd_ready = sem("rstd_ready")
    x1_ready = sem("x1_ready")
    x1T_ready = sem("x1T_ready")
    pool_passed = sem("pool_passed")
    dve_passed = sem("dve_passed")

    xv = t["x"].rearrange("(g b) l d -> l g b d", b=GB)
    NW = 12

    MISC_PRE = ["xT", "xb0", "xb1", "z0", "z1", "dtlow", "bc", "dt0", "dt1"]
    ACT_PRE = ["xT", "pad0", "xc0", "pad1", "xc1", "thz0", "th0", "thz1", "th1", "dtlow", "hi",
               "abs0", "mid_row", "abs1", "exp", "ln"]
    DVE_PRE = ["c00", "c01", "c02", "c10", "c11", "c12", "xb0", "z0", "xb1", "z1", "rest", "relu0",
               "low", "relu1", "dt", "dtx"]
    POOL_PRE = ["mid", "first"]

    def misc(name, g):
        return after(len(MISC_PRE), MISC_PRE.index(name), g)

    def apre(name, g):
        return after(len(ACT_PRE), ACT_PRE.index(name), g)

    def dpre(name, g):
        return after(len(DVE_PRE), DVE_PRE.index(name), g)

    def ppre(name, g):
        return after(len(POOL_PRE), POOL_PRE.index(name), g)

    tail_full = sem("tail_full")

    def over_groups(eng, group):
        group(0, 0, True, False)
        group(1, 1, False, False)
        with eng.Fori(1, NG // 2 - 1) as i:
            group(i * 2, 0, False, False)
            group(i * 2 + 1, 1, False, False)
        group(NG - 2, 0, False, False)
        group(NG - 1, 1, False, True)

    block = nc.Block()
    blk = block.__enter__()

    @blk.sync
    def _(sp):
        for dst, src in [
            (w_in[:], t["L0_attn_W_in"]),
            (conv_w[:], t["L0_attn_conv_w"].rearrange("(c p) k -> p c k", p=P)),
            (conv_b[:], t["L0_attn_conv_b"].rearrange("(c p) -> p c", p=P)),
            (w_dtlow[:], t["L0_attn_W_x"][:, 0:R].rearrange("(c p) k -> p c k", p=P)),
            (w_dt[:], t["L0_attn_W_dt"]),
            (b_dt[:], t["L0_attn_b_dt"].rearrange("(c p) -> p c", p=P)),
            (a_neg[:], t["L0_attn_A_log"].rearrange("(c p) n -> p c n", p=P)),
            (d_half[:], t["L0_attn_D"].rearrange("(c p) -> p c", p=P)),
            (w_out[:], t["L0_attn_W_out"].rearrange("(c p) d -> p c d", p=P)),
        ] + [(w_bc3[:, :, j, :], t["L0_attn_W_x"][:, R:].rearrange("(c p) k -> p c k", p=P)) for j in range(3)]:
            sp.dma_start(dst, src, allow_slow_non_contiguous=True).then_inc(w_loaded, 16)
        sp.dma_start(x_tok[:], xv[:, 0]).then_inc(x_loaded, 16)

        def group(g, par, first, last):
            if not last:
                sp.wait_ge(misc_full, misc("xT", g))
                sp.dma_start(x_tok[:], xv[:, bass.ds(g + 1, 1)].rearrange("l g b d -> l (g b) d")).then_inc(x_loaded, 16)
            if not first:
                sp.wait_ge(res_ready, g)
            sp.dma_start(x_res[:], xv[:, bass.ds(g, 1)].rearrange("l g b d -> l (g b) d")).then_inc(res_loaded, 16)
        over_groups(sp, group)

    @blk.gpsimd
    def _(pool):
        pool.memset(ident[:], 0.0).then_inc(consts_pool, 1)
        pool.memset(pick[:], 0.0).then_inc(consts_pool, 1)
        pool.memset(minus_half[:], -0.5).then_inc(consts_pool, 1)
        pool.memset(xb_pad[:], 0.0).then_inc(consts_pool, 1)
        pool.wait_ge(consts_pool, 4)
        pool.affine_select(out=ident[:], in_=ident[:], compare_op=ALU.not_equal, fill=1.0, base=0,
                           pattern=[[-1, P]], channel_multiplier=1).then_inc(consts_pool, 1)
        for j in range(3):
            pool.affine_select(out=pick[:], in_=pick[:], compare_op=ALU.not_equal, fill=1.0, base=-32 * j,
                               pattern=[[-1, 2 * NS], [0, P]], channel_multiplier=1).then_inc(consts_pool, 1)
            pool.wait_ge(consts_pool, 6 + j)

        def split_mid(g, par):
            hold(pool, dve_pre, dpre("rest", g), pool_passed)
            pool.tensor_copy(bc_mid[:], bc_rest[:]).then_inc(pool_pre, 1)

        def first_steps(g, par):
            hold(pool, dve_pre, dpre("dtx", g), pool_passed)
            pool.memset(dt[:, par].rearrange("p c (b l) -> p (c b) l", l=P)[:, :, 0:1], HUGE).then_inc(pool_pre, 1)

        split_mid(0, 0)
        first_steps(0, 0)

        def group(g, par, first, last):
            for n in range(NS):
                for c in range(C):
                    u = n * C + c
                    pool.wait_ge(state_ready, after(U, u, g))
                    if c == 0:
                        pool.wait_ge(c_ready, after(NS, n, g))
                    need(pool, y_added, after(U, u, g) - 4)
                    pool.tensor_tensor(hc[:, u % 4], state[:, u % 4], c_bc[:, n % 2], ALU.mult).then_inc(hc_ready, 1)
                if not last:
                    if n == 8:
                        split_mid(g + 1, 1 - par)
                    if n == 13:
                        first_steps(g + 1, 1 - par)
                if not first and n == 12:
                    pool.wait_ge(ln_step, after(3, 2, g - 1))
                    pool.tensor_tensor(rstd[:], veps[:], minus_half[:], ALU.pow).then_inc(rstd_ready, 1)
        over_groups(pool, group)
        pool.wait_ge(ln_step, after(3, 2, NG - 1))
        pool.tensor_tensor(rstd[:], veps[:], minus_half[:], ALU.pow).then_inc(rstd_ready, 1)

    @blk.scalar
    def _(act):
        act.wait_ge(w_loaded, 16 * NW)
        act.activation(a_neg[:], a_neg[:], ACT.Exp).then_inc(a_ready, 1)
        act.wait_ge(a_ready, 1)
        act.mul(a_neg[:], a_neg[:], -1.0).then_inc(a_ready, 1)
        act.wait_ge(a_ready, 2)
        act.wait_ge(w_scaled, 4)
        act.wait_ge(consts_pool, 8)

        def piece_xT(g, par):
            act.wait_ge(misc_full, misc("xT", g))
            act.copy(xT[:], ps_misc[:]).then_inc(act_pre, 1)

        def piece_xb(g, par, c):
            act.wait_ge(misc_full, misc(f"xb{c}", g))
            need(act, dve_pre, dpre(f"c{c}2", g - 1))
            act.copy(xb_pad[:, c, :, 3:], ps_misc[:].rearrange("p (b l) -> p b l", l=P)).then_inc(act_pre, 1)
            need(act, dve_pre, dpre(f"xb{c}", g - 1))
            act.activation(xc[:, c], ps_misc[:], ACT.Identity, bias=conv_b[:, c:c + 1], scale=conv_w[:, c, 3:4]).then_inc(act_pre, 1)

        def piece_th(g, par, c):
            act.wait_ge(misc_full, misc(f"z{c}", g))
            need(act, dve_pre, dpre(f"z{c}", g - 1))
            act.activation(thz[:, c], ps_misc[:], ACT.Tanh, scale=0.5).then_inc(act_pre, 1)
            act.wait_ge(dve_pre, dpre(f"c{c}2", g))
            act.activation(th[:, c], xc[:, c], ACT.Tanh, scale=0.5).then_inc(act_pre, 1)

        def piece_dtlow(g, par):
            act.wait_ge(misc_full, misc("dtlow", g))
            act.copy(dt_low[:], ps_misc[0:R]).then_inc(act_pre, 1)

        def piece_hi(g, par):
            act.wait_ge(misc_full, misc("bc", g))
            act.copy(bc_split[:, par], ps_misc[0:96]).then_inc(act_pre, 1)

        def piece_abs(g, par, c):
            act.wait_ge(misc_full, misc(f"dt{c}", g))
            need(act, dve_pre, dpre("dt", g - 1))
            act.activation(sp_abs[:, c], ps_misc[:], ACT.Abs, bias=b_dt[:, c:c + 1]).then_inc(act_pre, 1)

        def piece_exp(g, par):
            act.wait_ge(act_pre, apre("abs1", g))
            act.activation(sp_abs[:], sp_abs[:], ACT.Exp, scale=-1.0).then_inc(act_pre, 1)

        def piece_ln(g, par):
            act.wait_ge(act_pre, apre("exp", g))
            act.activation(sp_abs[:], sp_abs[:], ACT.Ln, bias=1.0).then_inc(act_pre, 1)

        def prepare(g, par, n):
            if n == 0:
                piece_xT(g, par)
            if n == 2:
                piece_xb(g, par, 0)
            if n == 3:
                piece_xb(g, par, 1)
            if n == 4:
                piece_th(g, par, 0)
            if n == 5:
                piece_th(g, par, 1)
            if n == 7:
                piece_dtlow(g, par)
            if n == 8:
                piece_hi(g, par)
            if n == 9:
                piece_abs(g, par, 0)
            if n == 10:
                act.wait_ge(pool_pre, ppre("mid", g))
                act.copy(bc_split[32:64, par], bc_mid[32:64]).then_inc(act_pre, 1)
                piece_abs(g, par, 1)
                piece_exp(g, par)
            if n == 11:
                piece_ln(g, par)

        def decay(g, par, n, c):
            u = n * C + c
            if u == 0:
                act.wait_ge(pool_pre, ppre("first", g))
            need(act, state_ready, after(U, u, g) - 2)
            act.activation(ps_da[u % 2][:], dt[:, par, c], ACT.Exp, scale=a_neg[:, c, n:n + 1]).then_inc(da_ready, 1)

        def copy_c(g, par, n):
            act.wait_ge(c_full, after(NS, n, g))
            need(act, hc_ready, after(U, n * C + 1, g) - 4)
            act.copy(c_bc[:, n % 2], ps_c[:]).then_inc(c_ready, 1)

        def finish(g):
            act.wait_ge(tail_full, after(2, 1, g))
            act.copy(x1T[:, bass.ds(g * T, T)], ps_misc[:]).then_inc(x1T_ready, 1)

        for n in range(NS):
            prepare(0, 0, n)
        copy_c(0, 0, 0)
        decay(0, 0, 0, 0)
        decay(0, 0, 0, 1)

        def group(g, par, first, last):
            for n in range(NS):
                if n < NS - 1:
                    copy_c(g, par, n + 1)
                    decay(g, par, n + 1, 0)
                if not last:
                    prepare(g + 1, 1 - par, n)
                if n < NS - 1:
                    decay(g, par, n + 1, 1)
                if not first and n == 15:
                    finish(g - 1)
            if not last:
                copy_c(g + 1, 1 - par, 0)
                decay(g + 1, 1 - par, 0, 0)
                decay(g + 1, 1 - par, 0, 1)
        over_groups(act, group)
        finish(NG - 1)

    @blk.vector
    def _(dve):
        dve.wait_ge(w_loaded, 16 * NW)
        dve.tensor_scalar_mul(w_dtlow[:], w_dtlow[:], 0.5).then_inc(w_scaled, 1)
        dve.tensor_scalar_mul(w_bc3[:], w_bc3[:], 0.5).then_inc(w_scaled, 1)
        dve.tensor_scalar_mul(d_half[:], d_half[:], 0.5).then_inc(w_scaled, 1)
        dve.tensor_scalar_mul(w_out[:], w_out[:], 0.5).then_inc(w_scaled, 1)
        dve.wait_ge(w_scaled, 4)

        def taps(g, c):
            for k in range(3):
                if k == 0:
                    dve.wait_ge(act_pre, apre(f"xc{c}", g))
                else:
                    dve.wait_ge(dve_pre, dpre(f"c{c}{k - 1}", g))
                v = xc[:, c].rearrange("p (b l) -> p b l", l=P)
                dve.scalar_tensor_tensor(v, xb_pad[:, c, :, k:k + P], conv_w[:, c, k:k + 1], v, ALU.mult, ALU.add).then_inc(dve_pre, 1)

        def silus(g, par, c):
            dve.wait_ge(act_pre, apre(f"th{c}", g))
            dve.scalar_tensor_tensor(xb2[:, par, c], th[:, c], 1.0, xc[:, c], ALU.add, ALU.mult).then_inc(dve_pre, 1)

        def zsilu(g, par, c):
            dve.wait_ge(act_pre, apre(f"thz{c}", g))
            dve.scalar_tensor_tensor(sz2[:, par, c], thz[:, c], 1.0, ps_misc[:], ALU.add, ALU.mult).then_inc(dve_pre, 1)

        def rest(g, par):
            dve.wait_ge(act_pre, apre("hi", g))
            need(dve, pool_pre, ppre("mid", g - 1))
            dve.tensor_tensor(bc_rest[:], ps_misc[0:96], bc_split[:, par], ALU.subtract).then_inc(dve_pre, 1)

        def low(g, par):
            dve.wait_ge(pool_pre, ppre("mid", g))
            dve.tensor_tensor(bc_split[64:96, par], bc_rest[64:96], bc_mid[64:96], ALU.subtract).then_inc(dve_pre, 1)

        def relu(g, par, c):
            dve.wait_ge(act_pre, apre(f"abs{c}", g))
            dve.tensor_scalar(sp_relu[:, c], ps_misc[:], b_dt[:, c:c + 1], 0.0, ALU.add, ALU.max).then_inc(dve_pre, 1)

        def dts(g, par):
            dve.wait_ge(act_pre, apre("ln", g))
            dve.wait_ge(dve_pre, dpre("relu1", g))
            dve.tensor_tensor(dt[:, par], sp_relu[:], sp_abs[:], ALU.add).then_inc(dve_pre, 1)

        def dtxs(g, par):
            dve.wait_ge(dve_pre, dpre("dt", g))
            dve.scalar_tensor_tensor(dtx[:, par], dt[:, par], 0.5, xb2[:, par], ALU.mult, ALU.mult).then_inc(dve_pre, 1)

        def prepare(g, par, n):
            if n == 3:
                taps(g, 0)
            if n == 4:
                taps(g, 1)
            if n == 5:
                silus(g, par, 0)
                zsilu(g, par, 0)
            if n == 6:
                silus(g, par, 1)
                zsilu(g, par, 1)
            if n == 8:
                rest(g, par)
            if n == 9:
                relu(g, par, 0)
                low(g, par)
            if n == 10:
                relu(g, par, 1)
            if n == 12:
                dts(g, par)
            if n == 13:
                dtxs(g, par)

        def tail(g, par, n):
            if n == 1:
                dve.wait_ge(y_added, after(U, U - 1, g))
                for c in range(C):
                    dve.scalar_tensor_tensor(yd[:, c], xb2[:, par, c], d_half[:, c:c + 1], ps_y[c][:], ALU.mult, ALU.add).then_inc(y_taken, 1)
            if n == 2:
                need(dve, tail_full, after(2, 0, g - 1))
                for c in range(C):
                    dve.wait_ge(y_taken, after(C, c, g))
                    dve.tensor_tensor(yz[:, c], yd[:, c], sz2[:, par, c], ALU.mult).then_inc(yz_ready, 1)
            if n == 11:
                dve.wait_ge(tail_full, after(2, 0, g))
                dve.wait_ge(res_loaded, 16 * g + 16)
                dve.tensor_tensor(res[:], ps_misc[:].rearrange("p (b d) -> p b d", d=P), x_res[:], ALU.add).then_inc(res_ready, 1)
                dve.wait_ge(res_ready, after(1, 0, g))
                for b in range(GB):
                    ins = dve.bn_stats(stats[:, b], res[:, b])
                ins.then_inc(ln_step, 1)
                hold(dve, ln_step, after(3, 0, g), dve_passed)
                for b in range(GB):
                    ins = dve.bn_aggr(mv[:, b], stats[:, b])
                ins.then_inc(ln_step, 1)
                dve.wait_ge(ln_step, after(3, 1, g))
                dve.tensor_scalar_add(veps[:], mv[:, :, 1], LN_EPS).then_inc(ln_step, 1)
            if n == 13:
                dve.wait_ge(rstd_ready, after(1, 0, g))
                for b in range(GB):
                    ins = dve.tensor_scalar(res[:, b], res[:, b], mv[:, b, 0:1], rstd[:, b:b + 1], ALU.subtract, ALU.mult)
                ins.then_inc(x1_ready, 1)

        def feed(g, par, n, c):
            u = n * C + c
            if u == 0:
                dve.wait_ge(dve_pre, dpre("dtx", g))
            if c == 0:
                dve.wait_ge(b_ready, after(NS, n, g))
            need(dve, state_ready, after(U, u, g) - 4)
            dve.tensor_tensor(inp[:, u % 4], dtx[:, par, c], ps_b[n % 2][:], ALU.mult).then_inc(inp_ready, 1)

        def scan(g, par, n, c):
            u = n * C + c
            dve.wait_ge(da_ready, after(U, u, g))
            dve.wait_ge(inp_ready, after(U, u, g))
            need(dve, hc_ready, after(U, u, g) - 4)
            dve.tensor_tensor_scan(state[:, u % 4], ps_da[u % 2][:], inp[:, u % 4], 0.0, ALU.mult, ALU.add).then_inc(state_ready, 1)

        for n in range(NS):
            prepare(0, 0, n)
        feed(0, 0, 0, 0)

        def group(g, par, first, last):
            for n in range(NS):
                feed(g, par, n, 1)
                scan(g, par, n, 0)
                if not last:
                    prepare(g + 1, 1 - par, n)
                if n < NS - 1:
                    feed(g, par, n + 1, 0)
                elif not last:
                    feed(g + 1, 1 - par, 0, 0)
                scan(g, par, n, 1)
                if not first:
                    tail(g - 1, 1 - par, n)
        over_groups(dve, group)
        for n in range(NS):
            tail(NG - 1, 1, n)

    @blk.tensor
    def _(pe):
        pe.wait_ge(w_loaded, 16 * NW)
        pe.wait_ge(w_scaled, 4)
        pe.wait_ge(consts_pool, 8)

        def fill_misc(g, par, name):
            if name == "xT":
                pe.wait_ge(x_loaded, 16 * g + 16)
                need(pe, dve_pre, dpre("relu1", g - 1))
                need(pe, x1T_ready, g - 2)
                for b in range(GB):
                    ins = pe.transpose(ps_misc[:, b * P:(b + 1) * P], x_tok[:, b], ident[:])
            if name in ("xb0", "xb1", "z0", "z1"):
                j = MISC_PRE.index(name) - 1
                if j <= 2:
                    pe.wait_ge(act_pre, apre(("xT", "xc0", "xc1")[j], g))
                if name == "z1":
                    pe.wait_ge(dve_pre, dpre("z0", g))
                ins = pe.matmul(ps_misc[:], w_in[:, j * P:(j + 1) * P], xT[:], start=True, stop=True)
            if name == "dtlow":
                pe.wait_ge(dve_pre, dpre("z1", g))
                for c in range(C):
                    ins = pe.matmul(ps_misc[0:R], w_dtlow[:, c], xb2[:, par, c], start=c == 0, stop=c == C - 1)
            if name == "bc":
                pe.wait_ge(act_pre, apre("dtlow", g))
                for c in range(C):
                    ins = pe.matmul(ps_misc[0:96], w_bc3[:, c].rearrange("p j k -> p (j k)"), xb2[:, par, c], start=c == 0, stop=c == C - 1)
            if name in ("dt0", "dt1"):
                c = int(name[2])
                pe.wait_ge(dve_pre, dpre(("rest", "relu0")[c], g))
                ins = pe.matmul(ps_misc[:], w_dt[:, c * P:(c + 1) * P], dt_low[:], start=True, stop=True)
            ins.then_inc(misc_full, 1)

        SLOT = {0: "xT", 1: "xb0", 2: "xb1", 3: "z0", 4: "z1", 6: "dtlow", 7: "bc", 8: "dt0", 9: "dt1"}

        def tail(g, n):
            if n == 10:
                pe.wait_ge(yz_ready, after(C, C - 1, g))
                for b in range(GB):
                    for c in range(C):
                        ins = pe.matmul(ps_misc[:, b * P:(b + 1) * P], yz[:, c, b * P:(b + 1) * P], w_out[:, c], start=c == 0, stop=c == C - 1)
                ins.then_inc(tail_full, 1)
            if n == 14:
                pe.wait_ge(x1_ready, after(1, 0, g))
                for b in range(GB):
                    ins = pe.transpose(ps_misc[:, b * P:(b + 1) * P], res[:, b], ident[:])
                ins.then_inc(tail_full, 1)

        def spread(g, par, n):
            if n == 0:
                pe.wait_ge(act_pre, apre("mid_row", g))
                pe.wait_ge(dve_pre, dpre("low", g))
            need(pe, inp_ready, after(U, n * C + 1, g) - 4)
            pe.matmul(ps_b[n % 2][:], pick[:, n], bc_split[:, par], start=True, stop=True).then_inc(b_ready, 1)
            need(pe, c_ready, after(NS, n, g) - 1)
            pe.matmul(ps_c[:], pick[:, NS + n], bc_split[:, par], start=True, stop=True).then_inc(c_full, 1)

        def add_y(g, n):
            for c in range(C):
                u = n * C + c
                pe.wait_ge(hc_ready, after(U, u, g))
                if n == 0:
                    need(pe, y_taken, after(C, c, g - 1))
                pe.matmul(ps_y[c][:], ident[:], hc[:, u % 4], start=n == 0, stop=n == NS - 1).then_inc(y_added, 1)

        for n in range(NS):
            if n in SLOT:
                fill_misc(0, 0, SLOT[n])
        spread(0, 0, 0)

        def group(g, par, first, last):
            for n in range(NS):
                if n < NS - 1:
                    spread(g, par, n + 1)
                elif not last:
                    spread(g + 1, 1 - par, 0)
                if n == 0 and not first:
                    add_y(g - 1, NS - 1)
                if n > 0:
                    add_y(g, n - 1)
                if not last and n in SLOT:
                    fill_misc(g + 1, 1 - par, SLOT[n])
                if not first and n == 10:
                    if last:
                        pe.wait_ge(x1T_ready, g - 1)
                    else:
                        pe.wait_ge(dve_pre, dpre("relu1", g + 1))
                if not first:
                    tail(g - 1, n)
        over_groups(pe, group)
        add_y(NG - 1, NS - 1)
        pe.wait_ge(x1T_ready, NG - 1)
        tail(NG - 1, 10)
        tail(NG - 1, 14)

    block.__exit__(None, None, None)


ITERS = 3


def slot_stage(nc, t, sb, psum, sem, x1T, x2, ident, NG):
    M = t["ctx_1024"].shape[1]
    NQ = NG // 2
    SCALE = float(P) ** -0.5
    ctx = sb("ctx", [M, 2, GB, P])
    ctx_sq = sb("ctx_sq", [M, P])
    ctx_ss = sb("ctx_ss", [M, 2, GB])
    ctx_r = sb("ctx_r", [M, 2, GB])
    pn = sb("pn", [M, GB, P])
    pnT = sb("pnT", [P, GB * M])
    kq = sb("kq", [P, 2, GB * M])
    vw = sb("vw", [M, 2, GB, 3 * P])
    wq = sb("wq", [P, P])
    wk = sb("wk", [P, P])
    wv = sb("wv", [P, P])
    wih = sb("wih", [P, 3, P])
    whh = sb("whh", [P, 3, P])
    w_slot = sb("w_slot", [P, 1])
    w_input = sb("w_input", [P, 1])
    bih = sb("bih", [P, 3])
    bhh = sb("bhh", [P, 3])
    bias = sb("bias", [P, 3])
    wihT = sb("wihT", [P, 3 * P])
    whhT = sb("whhT", [P, 3 * P])
    kq_w = sb("kq_w", [P, P])
    vw_w = sb("vw_w", [P, 3 * P])
    ones = sb("ones", [P, 1])
    m_half = sb("m_half", [P, GB])
    h = [sb(f"h{k}", [P, T]) for k in range(2)]
    sq = [sb(f"sq{k}", [P, T]) for k in range(2)]
    sn = [sb(f"sn{k}", [P, T]) for k in range(2)]
    ms = [sb(f"ms{k}", [P, GB]) for k in range(2)]
    rs = [sb(f"rs{k}", [P, GB]) for k in range(2)]
    mx = [sb(f"mx{k}", [M, GB]) for k in range(2)]
    nmx = [sb(f"nmx{k}", [M, GB]) for k in range(2)]
    ex = [sb(f"ex{k}", [M, T]) for k in range(2)]
    se = [sb(f"se{k}", [M, GB]) for k in range(2)]
    rse = [sb(f"rse{k}", [M, GB]) for k in range(2)]
    dn = [sb(f"dn{k}", [P, GB]) for k in range(2)]
    rdn = [sb(f"rdn{k}", [P, GB]) for k in range(2)]
    at = [sb(f"at{k}", [M, T]) for k in range(2)]
    hnb = sb("hnb", [P, T])
    tr = sb("tr", [P, T])
    tz = sb("tz", [P, T])
    nn = sb("nn", [P, T])
    rh = sb("rh", [P, T])
    pre = sb("pre", [P, T])
    df = sb("df", [P, T])
    zd = sb("zd", [P, T])
    res2 = [sb(f"res2_{k}", [P, T]) for k in range(2)]
    tok = [sb(f"tok{k}", [P, GB, P]) for k in range(2)]
    stats2 = [sb(f"stats2_{k}", [P, GB, 6]) for k in range(2)]
    mv2 = [sb(f"mv2_{k}", [P, GB, 2]) for k in range(2)]
    veps2 = [sb(f"veps2_{k}", [P, GB]) for k in range(2)]
    rstd2 = [sb(f"rstd2_{k}", [P, GB]) for k in range(2)]
    ps_s = [psum(f"ps_s{k}", [P, T]) for k in range(2)]
    ps_r = psum("ps_r", [P, T])
    ps_z = psum("ps_z", [P, T])
    ps_hn = psum("ps_hn", [P, T])
    ps_xn = psum("ps_xn", [P, T])
    ps_u = [psum(f"ps_u{k}", [P, T]) for k in range(2)]

    PE1 = ["ssq", "rbc", "scores", "den", "dbc"]
    PE2 = ["hn", "r", "z", "xn"]
    V = ["ms", "sn", "mx", "nmx", "rse", "dn", "rdn", "attn"]
    V2 = ["rh", "pre", "df", "zd", "h"]
    A2 = ["hnb", "tr", "tz", "nn"]
    POSTV = ["res2", "stats", "aggr", "veps", "x2"]
    loaded = sem("slot_w_loaded")
    const2 = sem("const2")
    prep_pe = sem("prep_pe")
    prep_act = sem("prep_act")
    prep_v = sem("prep_v")
    pe1 = [sem(f"pe1_{k}") for k in range(2)]
    pe2 = [sem(f"pe2_{k}") for k in range(2)]
    dve1 = [sem(f"dve1_{k}") for k in range(2)]
    dve2 = [sem(f"dve2_{k}") for k in range(2)]
    squared = [sem(f"squared{k}") for k in range(2)]
    exped = [sem(f"exped{k}") for k in range(2)]
    act2 = [sem(f"act2_{k}") for k in range(2)]
    rooted = [sem(f"rooted{k}") for k in range(2)]
    h_loaded = [sem(f"h_loaded{k}") for k in range(2)]
    post_v = [sem(f"post_v{k}") for k in range(2)]
    post_pe = [sem(f"post_pe{k}") for k in range(2)]
    post_act = [sem(f"post_act{k}") for k in range(2)]
    post_root = [sem(f"post_root{k}") for k in range(2)]
    ctx_loaded = [sem(f"ctx_loaded{k}") for k in range(2)]
    ctx_sumsq = [sem(f"ctx_sumsq{k}") for k in range(2)]
    ctx_ms = [sem(f"ctx_ms{k}") for k in range(2)]
    ctx_root = [sem(f"ctx_root{k}") for k in range(2)]
    ctx_normed = [sem(f"ctx_normed{k}") for k in range(2)]
    u_full = sem("u_full")
    u_read = sem("u_read")
    passed2 = [sem(f"passed2_{k}") for k in range(2)]

    def ev(names, name, it):
        return after(len(names), names.index(name), it)

    def u_value(i, beat, k):
        return 2 + i * 12 + {0: 0, 1: 6, 5: 10}[beat] + k + 1

    def over_pairs(eng, body):
        body(0, True, False)
        with eng.Fori(1, NQ - 1) as i:
            body(i, False, False)
        body(NQ - 1, False, True)

    def beats(i, attention, gru):
        for beat in range(2 * ITERS):
            j = beat // 2
            lane = beat % 2
            yield beat, (lane, i * ITERS + j, j), (1 - lane, i * ITERS + j - (1 - lane), j - (1 - lane))

    block = nc.Block()
    blk = block.__enter__()
    cview = t["ctx_1024"].rearrange("(q k b) m d -> m q k b d", k=2, b=GB)

    def ctx_of(q, k):
        return cview[:, bass.ds(q, 1), k].rearrange("m q b d -> m (q b) d")

    @blk.sync
    def _(sp):
        for dst, src in [
            (wq[:], t["L0_xattn_Wq"]), (wk[:], t["L0_xattn_Wk"]), (wv[:], t["L0_xattn_Wv"]),
            (wih[:], t["L0_xattn_gru_wih"].rearrange("(j p) d -> p j d", p=P)),
            (whh[:], t["L0_xattn_gru_whh"].rearrange("(j p) d -> p j d", p=P)),
            (w_slot[:], t["L0_xattn_slot_norm_w"].rearrange("(p o) -> p o", o=1)),
            (w_input[:], t["L0_xattn_input_norm_w"].rearrange("(p o) -> p o", o=1)),
            (bih[:], t["L0_xattn_gru_bih"].rearrange("(j p) -> p j", p=P)),
            (bhh[:], t["L0_xattn_gru_bhh"].rearrange("(j p) -> p j", p=P)),
        ]:
            sp.dma_start(dst, src, allow_slow_non_contiguous=True).then_inc(loaded, 16)
        for k in range(2):
            sp.dma_start(ctx[:, k], ctx_of(0, k)).then_inc(ctx_loaded[k], 16)

        def body(i, first, last):
            if not last:
                for k in range(2):
                    sp.wait_ge(ctx_normed[k], i + 1)
                    sp.dma_start(ctx[:, k], ctx_of(i + 1, k)).then_inc(ctx_loaded[k], 16)
        over_pairs(sp, body)

    @blk.gpsimd
    def _(pool):
        pool.memset(ones[:], 1.0).then_inc(const2, 1)
        pool.memset(m_half[:], -0.5).then_inc(const2, 1)
        pool.wait_ge(const2, 2)

        def norm_ctx(q, k):
            pool.wait_ge(ctx_ms[k], q + 1)
            pool.tensor_tensor(ctx_r[:, k], ctx_ss[:, k], m_half[0:M], ALU.pow).then_inc(ctx_root[k], 1)
            pool.wait_ge(ctx_root[k], q + 1)
            need(pool, u_full, (2 + 12 * q - 6 - 1) if k == 0 else (2 + 12 * q - 1))
            pool.tensor_tensor(pn[:], ctx[:, k], ctx_r[:, k].rearrange("m (b o) -> m b o", o=1).broadcast_to([M, GB, P]), ALU.mult).then_inc(ctx_normed[k], 1)

        def root(lane, it):
            pool.wait_ge(dve1[lane], ev(V, "ms", it))
            pool.tensor_tensor(rs[lane][:], ms[lane][:], m_half[:], ALU.pow).then_inc(rooted[lane], 1)

        def post_rooting(lane, q):
            pool.wait_ge(post_v[lane], ev(POSTV, "veps", q))
            pool.tensor_tensor(rstd2[lane][:], veps2[lane][:], m_half[:], ALU.pow).then_inc(post_root[lane], 1)

        norm_ctx(0, 0)

        def body(i, first, last):
            for beat, (a, it, _), _ in beats(i, None, None):
                if beat == 0:
                    norm_ctx(i, 1)
                root(a, it)
                if beat == 0 and not first:
                    post_rooting(0, i - 1)
                if beat == 1 and not first:
                    post_rooting(1, i - 1)
                if beat == 4 and not last:
                    norm_ctx(i + 1, 0)
        over_pairs(pool, body)
        post_rooting(0, NQ - 1)
        post_rooting(1, NQ - 1)

    @blk.scalar
    def _(act):
        act.wait_ge(loaded, 16 * 9)
        for j in range(2):
            act.wait_ge(prep_pe, j + 1)
            act.copy((wihT, whhT)[j][:], ps_u[j][:, 0:3 * P]).then_inc(prep_act, 1)
        act.wait_ge(prep_pe, 3)
        act.activation(kq_w[:], ps_u[0][:, 0:P], ACT.Copy, scale=w_input[:, 0:1]).then_inc(prep_act, 1)
        act.wait_ge(prep_pe, 4)
        act.activation(vw_w[:], ps_u[1][:, 0:3 * P], ACT.Copy, scale=w_input[:, 0:1]).then_inc(prep_act, 1)
        act.wait_ge(prep_v, 4)

        def sum_ctx(q, k):
            act.wait_ge(ctx_loaded[k], 16 * q + 16)
            need(act, ctx_root[k], q)
            for b in range(GB):
                if b:
                    act.wait_ge(ctx_sumsq[k], q * GB + b)
                elif isinstance(q, int) and q == 0 and k == 0:
                    pass
                else:
                    act.wait_ge(ctx_sumsq[1 - k], (q + (k - 1) + 1) * GB)
                act.activation(ctx_sq[:], ctx[:, k, b], ACT.Square, accum_out=ctx_ss[:, k, b:b + 1]).then_inc(ctx_sumsq[k], 1)

        def load_h(lane, q):
            if not (isinstance(q, int) and q == 0):
                act.wait_ge(post_v[lane], ev(POSTV, "res2", q - 1))
            g = q * 2 + lane
            act.copy(h[lane][:], x1T[:, bass.ds(g * T, T)]).then_inc(h_loaded[lane], 1)

        def context(i, beat):
            if beat in (0, 1):
                lane = beat
                for b in range(GB):
                    act.wait_ge(u_full, u_value(i, beat, b))
                    act.copy(vw[:, lane, b], ps_u[b % 2][0:M, 0:3 * P]).then_inc(u_read, 1)
            if beat in (0, 5):
                lane, k0 = (1, 4) if beat == 0 else (0, 0)
                act.wait_ge(u_full, u_value(i, beat, k0))
                act.copy(pnT[:], ps_u[0][:, 0:GB * M]).then_inc(u_read, 1)
                act.wait_ge(u_full, u_value(i, beat, k0 + 1))
                act.activation(kq[:, lane], ps_u[1][:, 0:GB * M], ACT.Copy, scale=w_slot[:, 0:1]).then_inc(u_read, 1)

        def attention_sq(lane, it, j, q):
            if j == 0:
                act.wait_ge(h_loaded[lane], q + 1)
            else:
                act.wait_ge(dve2[lane], ev(V2, "h", it - 1))
            act.activation(sq[lane][:], h[lane][:], ACT.Square).then_inc(squared[lane], 1)

        def attention_exp(lane, it):
            act.wait_ge(dve1[lane], ev(V, "nmx", it))
            for b in range(GB):
                act.activation(ex[lane][:, b * P:(b + 1) * P], ps_s[lane][0:M, b * P:(b + 1) * P], ACT.Exp,
                               bias=nmx[lane][:, b:b + 1], accum_out=se[lane][:, b:b + 1]).then_inc(exped[lane], 1)

        def gru(lane, it, other, oit):
            act.wait_ge(pe2[lane], ev(PE2, "hn", it))
            need(act, dve2[other], ev(V2, "rh", oit))
            act.activation(hnb[:], ps_hn[:], ACT.Identity, bias=bias[:, 2:3], scale=0.5).then_inc(act2[lane], 1)
            act.wait_ge(pe2[lane], ev(PE2, "r", it))
            act.activation(tr[:], ps_r[:], ACT.Tanh, bias=bias[:, 0:1], scale=0.5).then_inc(act2[lane], 1)
            act.wait_ge(pe2[lane], ev(PE2, "z", it))
            need(act, dve2[other], ev(V2, "zd", oit))
            act.activation(tz[:], ps_z[:], ACT.Tanh, bias=bias[:, 1:2], scale=0.5).then_inc(act2[lane], 1)

        def gru_n(lane, it, other, oit):
            act.wait_ge(dve2[lane], ev(V2, "pre", it))
            need(act, dve2[other], ev(V2, "h", oit))
            act.activation(nn[:], pre[:], ACT.Tanh, bias=bih[:, 2:3]).then_inc(act2[lane], 1)

        def post_read(lane, q):
            act.wait_ge(post_pe[lane], q + 1)
            need(act, post_v[lane], ev(POSTV, "x2", q - 1))
            act.copy(tok[lane][:].rearrange("p b d -> p (b d)"), ps_s[lane][:]).then_inc(post_act[lane], 1)

        sum_ctx(0, 0)
        act.wait_ge(u_full, 1)
        act.copy(pnT[:], ps_u[0][:, 0:GB * M]).then_inc(u_read, 1)
        act.wait_ge(u_full, 2)
        act.activation(kq[:, 0], ps_u[1][:, 0:GB * M], ACT.Copy, scale=w_slot[:, 0:1]).then_inc(u_read, 1)
        load_h(0, 0)
        load_h(1, 0)
        sum_ctx(0, 1)

        def body(i, first, last):
            for beat, (a, it, j), (b, it2, j2) in beats(i, None, None):
                attention_sq(a, it, j, i)
                if beat in (0, 1) and not first:
                    post_read(a, i - 1)
                if not (first and beat == 0):
                    gru(b, it2, 1 - b, it2 if b == 1 else it2 - 1)
                if beat == 5 and last:
                    pass
                elif beat in (0, 1, 5):
                    context(i, beat)
                if not (first and beat == 0):
                    gru_n(b, it2, 1 - b, it2 if b == 1 else it2 - 1)
                attention_exp(a, it)
                if beat == 0 and not first:
                    load_h(1, i)
                if beat == 5 and not last:
                    load_h(0, i + 1)
                if beat == 4 and not last:
                    sum_ctx(i + 1, 0)
                if beat == 5 and not last:
                    sum_ctx(i + 1, 1)
        over_pairs(act, body)
        it = NQ * ITERS - 1
        gru(1, it, 0, it)
        gru_n(1, it, 0, it)
        post_read(0, NQ - 1)
        post_read(1, NQ - 1)

    @blk.vector
    def _(dve):
        dve.wait_ge(loaded, 16 * 9)
        dve.tensor_tensor(bias[:, 0:2], bih[:, 0:2], bhh[:, 0:2], ALU.add).then_inc(prep_v, 1)
        dve.wait_ge(prep_v, 1)
        dve.tensor_scalar_mul(bias[:, 0:2], bias[:, 0:2], 0.5).then_inc(prep_v, 1)
        dve.tensor_scalar_mul(bias[:, 2:3], bhh[:, 2:3], 0.5).then_inc(prep_v, 1)
        dve.tensor_scalar_mul(w_slot[:], w_slot[:], SCALE).then_inc(prep_v, 1)

        def mean_ctx(q, k):
            dve.wait_ge(ctx_sumsq[k], q * GB + GB)
            dve.tensor_scalar(ctx_ss[:, k], ctx_ss[:, k], 1.0 / P, RMS_EPS, ALU.mult, ALU.add).then_inc(ctx_ms[k], 1)

        def mean_sq(lane, it):
            dve.wait_ge(pe1[lane], ev(PE1, "ssq", it))
            dve.tensor_scalar(ms[lane][:], ps_s[lane][:, 0:GB], 1.0 / P, RMS_EPS, ALU.mult, ALU.add).then_inc(dve1[lane], 1)

        def slots_normed(lane, it):
            dve.wait_ge(pe1[lane], ev(PE1, "rbc", it))
            dve.tensor_tensor(sn[lane][:], h[lane][:], ps_s[lane][:], ALU.mult).then_inc(dve1[lane], 1)

        def maxima(lane, it):
            dve.wait_ge(pe1[lane], ev(PE1, "scores", it))
            dve.reduce_max(mx[lane][:], ps_s[lane][0:M].rearrange("m (b s) -> m b s", b=GB), AX_X).then_inc(dve1[lane], 1)
            dve.wait_ge(dve1[lane], ev(V, "mx", it))
            dve.tensor_scalar_mul(nmx[lane][:], mx[lane][:], -1.0).then_inc(dve1[lane], 1)

        def normaliser(lane, it):
            dve.wait_ge(exped[lane], it * GB + GB)
            dve.reciprocal(rse[lane][:], se[lane][:]).then_inc(dve1[lane], 1)

        def denominators(lane, it):
            dve.wait_ge(pe1[lane], ev(PE1, "den", it))
            dve.tensor_scalar_add(dn[lane][:], ps_s[lane][:, 0:GB], RMS_EPS).then_inc(dve1[lane], 1)
            dve.wait_ge(dve1[lane], ev(V, "dn", it))
            dve.reciprocal(rdn[lane][:], dn[lane][:]).then_inc(dve1[lane], 1)

        def weights(lane, it):
            dve.wait_ge(pe1[lane], ev(PE1, "dbc", it))
            for b in range(GB):
                s = slice(b * P, (b + 1) * P)
                ins = dve.scalar_tensor_tensor(at[lane][:, s], ex[lane][:, s], rse[lane][:, b:b + 1], ps_s[lane][0:M, s], ALU.mult, ALU.mult)
            ins.then_inc(dve1[lane], 1)

        def gate_n(lane, it):
            dve.wait_ge(act2[lane], ev(A2, "tr", it))
            dve.scalar_tensor_tensor(rh[:], tr[:], 1.0, hnb[:], ALU.add, ALU.mult).then_inc(dve2[lane], 1)
            dve.wait_ge(dve2[lane], ev(V2, "rh", it))
            dve.wait_ge(pe2[lane], ev(PE2, "xn", it))
            dve.tensor_tensor(pre[:], rh[:], ps_xn[:], ALU.add).then_inc(dve2[lane], 1)

        def new_h(lane, it):
            dve.wait_ge(act2[lane], ev(A2, "nn", it))
            dve.tensor_tensor(df[:], h[lane][:], nn[:], ALU.subtract).then_inc(dve2[lane], 1)
            dve.wait_ge(dve2[lane], ev(V2, "df", it))
            dve.scalar_tensor_tensor(zd[:], tz[:], 1.0, df[:], ALU.add, ALU.mult).then_inc(dve2[lane], 1)
            dve.wait_ge(dve2[lane], ev(V2, "zd", it))
            dve.scalar_tensor_tensor(h[lane][:], zd[:], 0.5, nn[:], ALU.mult, ALU.add).then_inc(dve2[lane], 1)

        def residual(lane, q):
            dve.wait_ge(dve2[lane], ev(V2, "h", q * ITERS + ITERS - 1))
            g = q * 2 + lane
            dve.tensor_tensor(res2[lane][:], h[lane][:], x1T[:, bass.ds(g * T, T)], ALU.add).then_inc(post_v[lane], 1)

        def statistics(lane, q):
            dve.wait_ge(post_act[lane], q + 1)
            for b in range(GB):
                ins = dve.bn_stats(stats2[lane][:, b], tok[lane][:, b])
            ins.then_inc(post_v[lane], 1)
            hold(dve, post_v[lane], ev(POSTV, "stats", q), passed2[0])
            for b in range(GB):
                ins = dve.bn_aggr(mv2[lane][:, b], stats2[lane][:, b])
            ins.then_inc(post_v[lane], 1)
            dve.wait_ge(post_v[lane], ev(POSTV, "aggr", q))
            dve.tensor_scalar_add(veps2[lane][:], mv2[lane][:, :, 1], LN_EPS).then_inc(post_v[lane], 1)

        def normed(lane, q):
            dve.wait_ge(post_root[lane], q + 1)
            g = q * 2 + lane
            for b in range(GB):
                ins = dve.tensor_scalar(x2[:, bass.ds(g * GB + b, 1), :].rearrange("p o d -> p (o d)"), tok[lane][:, b],
                                        mv2[lane][:, b, 0:1], rstd2[lane][:, b:b + 1], ALU.subtract, ALU.mult)
            ins.then_inc(post_v[lane], 1)

        mean_ctx(0, 0)
        mean_ctx(0, 1)

        def body(i, first, last):
            for beat, (a, it, j), (b, it2, j2) in beats(i, None, None):
                working = not (first and beat == 0)
                mean_sq(a, it)
                if working:
                    gate_n(b, it2)
                slots_normed(a, it)
                if working:
                    new_h(b, it2)
                maxima(a, it)
                if beat in (0, 1) and not first:
                    statistics(a, i - 1)
                if beat == 0 and not first:
                    residual(1, i - 1)
                if beat == 5:
                    residual(0, i)
                normaliser(a, it)
                denominators(a, it)
                if beat in (0, 1) and not first:
                    normed(a, i - 1)
                weights(a, it)
                if beat == 4 and not last:
                    mean_ctx(i + 1, 0)
                if beat == 5 and not last:
                    mean_ctx(i + 1, 1)
        over_pairs(dve, body)
        it = NQ * ITERS - 1
        gate_n(1, it)
        new_h(1, it)
        residual(1, NQ - 1)
        for lane in range(2):
            statistics(lane, NQ - 1)
            normed(lane, NQ - 1)

    @blk.tensor
    def _(pe):
        pe.wait_ge(loaded, 16 * 9)
        for j, w in enumerate((wih, whh)):
            for k in range(3):
                ins = pe.transpose(ps_u[j][:, k * P:(k + 1) * P], w[:, k], ident[:])
            ins.then_inc(prep_pe, 1)
        pe.wait_ge(prep_act, 1)
        pe.matmul(ps_u[0][:, 0:P], wk[:], wq[:], start=True, stop=True).then_inc(prep_pe, 1)
        pe.wait_ge(prep_act, 2)
        pe.matmul(ps_u[1][:, 0:3 * P], wv[:], wihT[:], start=True, stop=True).then_inc(prep_pe, 1)
        pe.wait_ge(prep_act, 4)
        pe.wait_ge(const2, 2)

        def ctx_transposed(q, k):
            pe.wait_ge(ctx_normed[k], q + 1)
            for b in range(GB):
                ins = pe.transpose(ps_u[0][:, b * M:(b + 1) * M], pn[:, b], ident[0:M, 0:M])
            ins.then_inc(u_full, 1)

        def make_kq():
            pe.matmul(ps_u[1][:, 0:GB * M], kq_w[:], pnT[:], start=True, stop=True).then_inc(u_full, 1)

        def context(i, beat):
            if beat in (0, 1):
                for b in range(GB):
                    pe.wait_ge(u_read, u_value(i, beat, b) - (1 if b == 0 else 2))
                    pe.matmul(ps_u[b % 2][0:M, 0:3 * P], pnT[:, b * M:(b + 1) * M], vw_w[:], start=True, stop=True).then_inc(u_full, 1)
            if beat in (0, 5):
                lane, k0 = (1, 4) if beat == 0 else (0, 0)
                pe.wait_ge(u_read, u_value(i, beat, k0) - 2)
                ctx_transposed(i if beat == 0 else i + 1, lane)
                pe.wait_ge(u_read, u_value(i, beat, k0))
                make_kq()

        def ssq(lane, it):
            pe.wait_ge(squared[lane], it + 1)
            need(pe, dve1[lane], ev(V, "attn", it - 1))
            for b in range(GB):
                ins = pe.matmul(ps_s[lane][:, b:b + 1], sq[lane][:, b * P:(b + 1) * P], ones[:], start=True, stop=True)
            ins.then_inc(pe1[lane], 1)

        def root_spread(lane, it):
            pe.wait_ge(rooted[lane], it + 1)
            for b in range(GB):
                ins = pe.matmul(ps_s[lane][:, b * P:(b + 1) * P], rs[lane][:, b:b + 1].broadcast_to([P, P]), ident[:], start=True, stop=True)
            ins.then_inc(pe1[lane], 1)

        def scores(lane, it):
            pe.wait_ge(dve1[lane], ev(V, "sn", it))
            for b in range(GB):
                ins = pe.matmul(ps_s[lane][0:M, b * P:(b + 1) * P], kq[:, lane, b * M:(b + 1) * M], sn[lane][:, b * P:(b + 1) * P], start=True, stop=True)
            ins.then_inc(pe1[lane], 1)

        def den(lane, it):
            pe.wait_ge(dve1[lane], ev(V, "rse", it))
            for b in range(GB):
                ins = pe.matmul(ps_s[lane][:, b:b + 1], ex[lane][:, b * P:(b + 1) * P], rse[lane][:, b:b + 1], start=True, stop=True)
            ins.then_inc(pe1[lane], 1)

        def den_spread(lane, it):
            pe.wait_ge(dve1[lane], ev(V, "rdn", it))
            for b in range(GB):
                ins = pe.matmul(ps_s[lane][0:M, b * P:(b + 1) * P], rdn[lane][:, b:b + 1].broadcast_to([P, M]), ident[:], start=True, stop=True)
            ins.then_inc(pe1[lane], 1)

        def gates_h(lane, it, q, j, other, oit):
            if j == 0:
                pe.wait_ge(h_loaded[lane], q + 1)
            need(pe, act2[other], ev(A2, "hnb", oit))
            pe.matmul(ps_hn[:], whhT[:, 2 * P:], h[lane][:], start=True, stop=True).then_inc(pe2[lane], 1)
            need(pe, act2[other], ev(A2, "tz", oit))
            pe.matmul(ps_r[:], whhT[:, 0:P], h[lane][:], start=True, stop=False, skip_group_check=True)
            pe.matmul(ps_z[:], whhT[:, P:2 * P], h[lane][:], start=True, stop=False, skip_group_check=True)

        def gates_x(lane, it, q, j, other, oit):
            pe.wait_ge(dve1[lane], ev(V, "attn", it))
            if j == 0:
                pe.wait_ge(u_read, u_value(q, lane, GB - 1))
            for k, bank in enumerate((ps_r, ps_z, ps_xn)):
                if k == 2:
                    need(pe, dve2[other], ev(V2, "pre", oit))
                for b in range(GB):
                    ins = pe.matmul(bank[:, b * P:(b + 1) * P], vw[:, lane, b, k * P:(k + 1) * P], at[lane][:, b * P:(b + 1) * P],
                                    start=k == 2, stop=k == 2 or b == GB - 1, skip_group_check=True)
                ins.then_inc(pe2[lane], 1)

        def post(lane, q):
            pe.wait_ge(post_v[lane], ev(POSTV, "res2", q))
            need(pe, dve1[lane], ev(V, "attn", (q + 1) * ITERS - 1))
            for b in range(GB):
                ins = pe.transpose(ps_s[lane][:, b * P:(b + 1) * P], res2[lane][:, b * P:(b + 1) * P], ident[:])
            ins.then_inc(post_pe[lane], 1)

        ctx_transposed(0, 0)
        pe.wait_ge(u_read, 1)
        make_kq()

        def body(i, first, last):
            for beat, (a, it, j), (b, it2, j2) in beats(i, None, None):
                if beat in (0, 1) and not first:
                    post(a, i - 1)
                    pe.wait_ge(post_act[a], i)
                ssq(a, it)
                if not (first and beat == 0):
                    gates_x(b, it2, i if j2 >= 0 else i - 1, j2, 1 - b, it2 if b == 1 else it2 - 1)
                root_spread(a, it)
                if j == 0:
                    pe.wait_ge(u_read, u_value(i, 0, 5) if a == 1 else u_value(i, 0, 0) - 1)
                scores(a, it)
                if beat in (0, 1) or (beat == 5 and not last):
                    context(i, beat)
                gates_h(a, it, i, j, 1 - a, it2)
                den(a, it)
                den_spread(a, it)
        over_pairs(pe, body)
        it = NQ * ITERS - 1
        gates_x(1, it, NQ - 1, ITERS - 1, 0, it)
        for lane in range(2):
            post(lane, NQ - 1)

    block.__exit__(None, None, None)


ROWS = 256


def expert_stage(nc, t, sb, psum, sem, x2, ident, out):
    B = x2.shape[1]
    NE = t["L0_ffn_Wr"].shape[1]
    FF = t["L0_ffn_W1"].shape[2]
    FC = FF // P
    NG = B // GB
    NJ = (B * P + NE * (ROWS - 1)) // ROWS
    HALVES = ROWS // P
    assert NJ % 2 == 1 and FC == 4 and B * NE == 512
    xs = nc.dram_tensor("sorted_x", [NJ * ROWS, P], F32).ap()
    ys = nc.dram_tensor("sorted_y", [NJ * ROWS, P], F32).ap()
    w_r = sb("w_r", [P, NE])
    b_r = sb("b_r", [P, NE])
    zero = sb("zero", [P, P])
    all_ones = sb("all_ones", [P, P])
    before = sb("before", [P, P])
    e_index = sb("e_index", [P, NE])
    j_index = sb("j_index", [P, NJ])
    m_half3 = sb("m_half3", [P, GB])
    carry = sb("carry", [P, NE, B])
    x2T = sb("x2T", [P, 2, T])
    x_stage = sb("x_stage", [P, 2, GB, P])
    route = sb("route", [P, B, NE])
    gate = sb("gate", [P, B])
    cand = sb("cand", [P, B, NE])
    which = sb("which", [P, B])
    one_hot = sb("one_hot", [P, NE, B])
    totals = sb("totals", [P, NE, B])
    upto = sb("upto", [P, NE, B])
    place = sb("place", [P, NE, B])
    count_i = sb("count_i", [P, NE], I32)
    tiles = sb("tiles", [P, NE])
    tiles_end = sb("tiles_end", [P, NE])
    start = sb("start", [P, NE])
    dest_f = sb("dest_f", [P, B])
    dest = sb("dest", [P, B], I32)
    ended = sb("ended", [P, NJ, NE])
    tile_e = sb("tile_e", [P, NJ])
    expert = sb("expert", [P, NJ], I32)
    w1 = sb("w1", [P, 2, FF])
    w2 = sb("w2", [P, 2, FC, P])
    xrow = sb("xrow", [P, 2, HALVES, P])
    xcol = sb("xcol", [P, 2, ROWS])
    act_h = sb("act_h", [P, 2, FC, ROWS])
    yrow = sb("yrow", [P, 2, HALVES, P])
    yg = sb("yg", [P, B, P])
    stats3 = sb("stats3", [P, 2, GB, 6])
    mv3 = sb("mv3", [P, 2, GB, 2])
    veps3 = sb("veps3", [P, 2, GB])
    rstd3 = sb("rstd3", [P, 2, GB])
    fin = sb("fin", [P, 2, GB, P])
    ps_t = [psum(f"ps_t{k}", [P, T]) for k in range(2)]
    ps_h = [[psum(f"ps_h{k}{m}", [P, T]) for m in range(2)] for k in range(2)]
    ps_l = psum("ps_l", [P, T])
    ps_yy = psum("ps_yy", [P, T])

    loaded3 = sem("loaded3")
    const3 = sem("const3")
    const_v = sem("const_v")
    cleared = sem("cleared")
    staged = sem("staged")
    t_full = sem("t_full")
    t_read = sem("t_read")
    logits_done = sem("logits_done")
    summed = sem("summed")
    sigmoids = sem("sigmoids")
    step = sem("step")
    scattered = sem("scattered")
    tile_in = [sem(f"tile_in{k}") for k in range(2)]
    xcol_full = sem("xcol_full")
    xcol_read = sem("xcol_read")
    h_full = sem("h_full")
    h_act = sem("h_act")
    y_full = sem("y_full")
    y_read = sem("y_read")
    y_stored = [sem(f"y_stored{k}") for k in range(2)]
    gathered = [sem(f"gathered{k}") for k in range(2)]
    fin_step = sem("fin_step")
    fin_root = sem("fin_root")
    fin_done = sem("fin_done")
    stored = [sem(f"stored{k}") for k in range(2)]
    passed3 = sem("passed3")
    N_STEPS = 17

    block = nc.Block()
    blk = block.__enter__()

    def over_tiles(eng, tile):
        tile(0, 0)
        tile(1, 1)
        tile(2, 0)
        with eng.Fori(1, NJ // 2) as i:
            tile(i * 2 + 1, 1)
            tile(i * 2 + 2, 0)

    ov = out.rearrange("(g b) l d -> l g b d", b=GB)

    @blk.sync
    def _(sp):
        sp.dma_start(w_r[:], t["L0_ffn_Wr"]).then_inc(loaded3, 16)
        sp.dma_start(b_r[:], t["L0_ffn_br"].rearrange("(o e) -> o e", o=1).broadcast_to([P, NE])).then_inc(loaded3, 16)
        sp.wait_ge(const3, 1)
        sp.dma_start(xs.rearrange("(k p) d -> p k d", p=P),
                     zero[:].rearrange("p (o d) -> p o d", o=1).broadcast_to([P, NJ * HALVES, P])).then_inc(cleared, 16)
        sp.wait_ge(step, N_STEPS)
        sp.wait_ge(scattered, 16 * B)

        def store(j, par):
            sp.wait_ge(y_read, j + 1)
            sp.dma_start(ys[bass.ds(j * ROWS, ROWS)].rearrange("(s p) d -> p s d", p=P), yrow[:, par]).then_inc(y_stored[par], 16)

        def tile(j, par):
            need(sp, y_full, j - 1)
            e = sp.value_load(expert[0:1, bass.ds(j, 1)], min_val=0, max_val=NE - 1)
            sp.dma_start(w1[:, par], t["L0_ffn_W1"][bass.ds(e, 1)].rearrange("e d f -> d (e f)")).then_inc(tile_in[par], 16)
            sp.dma_start(w2[:, par], t["L0_ffn_W2"][bass.ds(e, 1)].rearrange("e (c p) d -> p (e c) d", p=P)).then_inc(tile_in[par], 16)
            sp.dma_start(xrow[:, par], xs[bass.ds(j * ROWS, ROWS)].rearrange("(s p) d -> p s d", p=P)).then_inc(tile_in[par], 16)
            if not isinstance(j, int) or j >= 2:
                store(j - 2, par)
        over_tiles(sp, tile)
        store(NJ - 2, 1)
        store(NJ - 1, 0)
        with sp.Fori(0, NG // 2) as i:
            for par in range(2):
                g = i * 2 + par
                sp.wait_ge(fin_done, g + 1)
                sp.dma_start(ov[:, bass.ds(g, 1)].rearrange("l g b d -> l (g b) d"), fin[:, par]).then_inc(stored[par], 16)
        for par in range(2):
            sp.wait_ge(stored[par], 16 * NG // 2)

    @blk.gpsimd
    def _(pool):
        pool.memset(zero[:], 0.0).then_inc(const3, 1)
        pool.memset(all_ones[:], 1.0).then_inc(const3, 1)
        pool.memset(m_half3[:], -0.5).then_inc(const3, 1)
        pool.memset(carry[:], 1.0).then_inc(const3, 1)
        pool.iota(e_index[:], pattern=[[1, NE]], base=0, channel_multiplier=0, allow_small_or_imprecise_dtypes=True).then_inc(const3, 1)
        pool.iota(j_index[:], pattern=[[1, NJ]], base=0, channel_multiplier=0, allow_small_or_imprecise_dtypes=True).then_inc(const3, 1)
        pool.wait_ge(const3, 6)
        pool.memset(carry[:, :, 0:1], 0.0).then_inc(const3, 1)
        pool.affine_select(out=before[:], in_=all_ones[:], compare_op=ALU.is_gt, fill=0.0, base=0,
                           pattern=[[1, P]], channel_multiplier=-1).then_inc(const3, 1)
        pool.wait_ge(cleared, 16)
        pool.wait_ge(step, N_STEPS)
        for b in range(B):
            pool.indirect_dma_start(xs, bass.IndirectOffsetOnAxis(ap=dest[:, b:b + 1], axis=0), x2[:, b, :], None).then_inc(scattered, 16)
        for par in range(2):
            pool.wait_ge(y_stored[par], 16 * (NJ // 2 + 1 - par))
        for g in range(NG):
            par = g % 2
            if g >= 2:
                pool.wait_ge(gathered[par], 16 * GB * (g // 2))
            for b in range(g * GB, (g + 1) * GB):
                pool.indirect_dma_start(yg[:, b, :], None, ys, bass.IndirectOffsetOnAxis(ap=dest[:, b:b + 1], axis=0)).then_inc(gathered[par], 16)
            if g >= 2:
                pool.wait_ge(fin_step, 4 * (g - 2) + 4)
                pool.tensor_tensor(rstd3[:, par], veps3[:, par], m_half3[:], ALU.pow).then_inc(fin_root, 1)
        for g in range(NG, NG + 2):
            pool.wait_ge(fin_step, 4 * (g - 2) + 4)
            pool.tensor_tensor(rstd3[:, g % 2], veps3[:, g % 2], m_half3[:], ALU.pow).then_inc(fin_root, 1)

    @blk.scalar
    def _(act):
        with act.Fori(0, NG // 2) as i:
            for par in range(2):
                g = i * 2 + par
                act.wait_ge(t_full, g + 1)
                act.copy(x2T[:, par], ps_t[par][:]).then_inc(t_read, 1)
        act.wait_ge(step, 1)
        act.activation(route[:], route[:], ACT.Sigmoid).then_inc(sigmoids, 1)

        def tile(j, par):
            for m in range(2):
                act.wait_ge(h_full, j * 2 + m + 1)
                if m == 0:
                    need(act, y_full, j - 1)
                act.activation(act_h[:, par, 2 * m:2 * m + 2].rearrange("p c r -> p (c r)"), ps_h[par][m][:], ACT.Gelu).then_inc(h_act, 1)
        over_tiles(act, tile)

    @blk.vector
    def _(dve):
        done = [0]

        def link(ins):
            done[0] += 1
            ins.then_inc(step, 1)
            dve.wait_ge(step, done[0])

        def over_b(ap, n):
            return ap.rearrange("p (o e) -> p o e", o=1).broadcast_to([P, n, NE])

        def over_e(ap):
            return ap.rearrange("p (b o) -> p b o", o=1).broadcast_to([P, B, NE])

        def stage_group(g, par, first):
            if not first:
                dve.wait_ge(t_full, g - 1)
            dve.tensor_copy(x_stage[:, par], x2[:, bass.ds(g * GB, GB)]).then_inc(staged, 1)
        stage_group(0, 0, True)
        stage_group(1, 1, True)
        with dve.Fori(1, NG // 2) as i:
            stage_group(i * 2, 0, False)
            stage_group(i * 2 + 1, 1, False)
        dve.wait_ge(loaded3, 32)
        dve.wait_ge(const3, 8)
        dve.wait_ge(logits_done, NG)
        link(dve.tensor_tensor(route[:], ps_l[:].rearrange("p (b e) -> p b e", e=NE), over_b(b_r[:], B), ALU.add))
        dve.wait_ge(sigmoids, 1)
        link(dve.reduce_max(gate[:], route[:], AX_X))
        link(dve.tensor_tensor(cand[:], route[:], over_e(gate[:]), ALU.is_lt))
        link(dve.scalar_tensor_tensor(cand[:], cand[:], float(NE), over_b(e_index[:], B), ALU.mult, ALU.add))
        link(dve.tensor_reduce(which[:], cand[:], AX_X, ALU.min))
        link(dve.tensor_tensor(one_hot[:].rearrange("p e b -> p b e"), over_b(e_index[:], B), over_e(which[:]), ALU.is_equal))
        dve.wait_ge(summed, 2)
        flat = "p e b -> p (e b)"
        link(dve.tensor_copy(totals[:].rearrange(flat), ps_t[1][:]))
        link(dve.tensor_tensor_scan(upto[:].rearrange(flat), carry[:].rearrange(flat), totals[:].rearrange(flat), 0.0, ALU.mult, ALU.add))
        link(dve.tensor_scalar_add(count_i[:], upto[:, :, B - 1], float(ROWS - 1)))
        link(dve.tensor_single_scalar(count_i[:], count_i[:], ROWS.bit_length() - 1, ALU.logical_shift_right))
        link(dve.tensor_copy(tiles[:], count_i[:]))
        link(dve.tensor_tensor_scan(tiles_end[:], all_ones[:, 0:NE], tiles[:], 0.0, ALU.mult, ALU.add))
        dve.tensor_tensor(start[:], tiles_end[:], tiles[:], ALU.subtract).then_inc(const_v, 1)
        dve.tensor_tensor(upto[:], upto[:], totals[:], ALU.subtract).then_inc(const_v, 1)
        dve.tensor_tensor(ended[:], over_b(tiles_end[:], NJ), j_index[:].rearrange("p (j o) -> p j o", o=1).broadcast_to([P, NJ, NE]), ALU.is_le).then_inc(const_v, 1)
        dve.wait_ge(const_v, 3)
        dve.tensor_reduce(tile_e[:], ended[:], AX_X, ALU.add).then_inc(const_v, 1)
        dve.tensor_tensor(place[:].rearrange(flat), upto[:].rearrange(flat), ps_t[0][:], ALU.add).then_inc(const_v, 1)
        dve.wait_ge(const_v, 5)
        dve.tensor_scalar(expert[:], tile_e[:], float(NE - 1), None, ALU.min).then_inc(const_v, 1)
        link(dve.scalar_tensor_tensor(place[:], start[:].rearrange("p (e o) -> p e o", o=1).broadcast_to([P, NE, B]), float(ROWS), place[:], ALU.mult, ALU.add))
        link(dve.tensor_tensor(place[:], place[:], one_hot[:], ALU.mult))
        link(dve.tensor_reduce(dest_f[:], place[:].rearrange("p e b -> p b e"), AX_X, ALU.add))
        dve.wait_ge(const_v, 6)
        link(dve.tensor_copy(dest[:], dest_f[:]))
        link(dve.memset(stats3[:], 0.0))
        assert done[0] == N_STEPS

        def tile(j, par):
            dve.wait_ge(xcol_full, j + 1)
            dve.tensor_copy(xcol[:, par], ps_t[par][:, 0:ROWS]).then_inc(xcol_read, 1)
            if not (isinstance(j, int) and j == 0):
                store_y(j - 1, 1 - par)

        def store_y(j, par):
            dve.wait_ge(y_full, j + 1)
            if not isinstance(j, int):
                dve.wait_ge(y_stored[par], stored_count(par))
            elif j >= 2:
                dve.wait_ge(y_stored[par], (j - par) // 2 * 16)
            dve.tensor_copy(yrow[:, par].rearrange("p s d -> p (s d)"), ps_yy[:, 0:ROWS]).then_inc(y_read, 1)

        pair = [None]

        def stored_count(par):
            return pair[0] * 16

        tile(0, 0)
        tile(1, 1)
        tile(2, 0)
        with dve.Fori(1, NJ // 2) as i:
            pair[0] = i
            tile(i * 2 + 1, 1)
            tile(i * 2 + 2, 0)
        store_y(NJ - 1, 0)

        def finish_pair(i, first):
            for par in range(2):
                g = i * 2 + par
                dve.wait_ge(gathered[par], i * (16 * GB) + 16 * GB)
                for b in range(GB):
                    s = g * GB + b
                    ins = dve.scalar_tensor_tensor(yg[:, bass.ds(s, 1)].rearrange("p o d -> p (o d)"), yg[:, bass.ds(s, 1)].rearrange("p o d -> p (o d)"),
                                                   gate[:, bass.ds(s, 1)], x2[:, bass.ds(s, 1)].rearrange("p o d -> p (o d)"), ALU.mult, ALU.add)
                ins.then_inc(fin_step, 1)
                hold(dve, fin_step, g * 4 + 1, passed3)
                for b in range(GB):
                    ins = dve.bn_stats(stats3[:, par, b], yg[:, bass.ds(g * GB + b, 1)].rearrange("p o d -> p (o d)"))
                ins.then_inc(fin_step, 1)
                hold(dve, fin_step, g * 4 + 2, passed3)
                for b in range(GB):
                    ins = dve.bn_aggr(mv3[:, par, b], stats3[:, par, b])
                ins.then_inc(fin_step, 1)
                dve.wait_ge(fin_step, g * 4 + 3)
                dve.tensor_scalar_add(veps3[:, par], mv3[:, par, :, 1], LN_EPS).then_inc(fin_step, 1)
                dve.wait_ge(fin_root, g + 1)
                if not first:
                    dve.wait_ge(stored[par], i * 16)
                for b in range(GB):
                    ins = dve.tensor_scalar(fin[:, par, b], yg[:, bass.ds(g * GB + b, 1)].rearrange("p o d -> p (o d)"),
                                            mv3[:, par, b, 0:1], rstd3[:, par, b:b + 1], ALU.subtract, ALU.mult)
                ins.then_inc(fin_done, 1)

        finish_pair(0, True)
        with dve.Fori(1, NG // 2) as i:
            finish_pair(i, False)

    @blk.tensor
    def _(pe):
        pe.wait_ge(loaded3, 32)
        def group(g, par, first):
            if not first:
                pe.wait_ge(t_read, g - 1)
            pe.wait_ge(staged, g + 1)
            for b in range(GB):
                ins = pe.transpose(ps_t[par][:, b * P:(b + 1) * P], x_stage[:, par, b], ident[:])
            ins.then_inc(t_full, 1)
            pe.wait_ge(t_read, g + 1)
            for b in range(GB):
                ins = pe.matmul(ps_l[:, bass.ds(g * (GB * NE) + b * NE, NE)], x2T[:, par, b * P:(b + 1) * P], w_r[:], start=True, stop=True)
            ins.then_inc(logits_done, 1)
        group(0, 0, True)
        group(1, 1, True)
        with pe.Fori(1, NG // 2) as i:
            group(i * 2, 0, False)
            group(i * 2 + 1, 1, False)
        pe.wait_ge(const3, 8)
        pe.wait_ge(step, 6)
        hot = one_hot[:].rearrange("p e b -> p (e b)")
        pe.matmul(ps_t[0][:], before[:], hot, start=True, stop=True).then_inc(summed, 1)
        pe.matmul(ps_t[1][:], all_ones[:], hot, start=True, stop=True).then_inc(summed, 1)
        pe.wait_ge(step, N_STEPS)

        def transposed(j, par):
            pe.wait_ge(tile_in[par], tile_count(j, par))
            need(pe, xcol_read, j - 1)
            for s in range(HALVES):
                ins = pe.transpose(ps_t[par][:, s * P:(s + 1) * P], xrow[:, par, s], ident[:])
            ins.then_inc(xcol_full, 1)

        def tile_count(j, par):
            return (j - par) // 2 * 48 + 48 if isinstance(j, int) else pair_count(par)

        pair = [None]

        def pair_count(par):
            return pair[0] * 48 + (48 if par else 96)

        def up(j, par):
            pe.wait_ge(xcol_read, j + 1)
            for m in range(2):
                need(pe, h_act, j * 2 - 4 + m + 1)
                for k in range(2):
                    c = 2 * m + k
                    ins = pe.matmul(ps_h[par][m][:, k * ROWS:(k + 1) * ROWS], w1[:, par, c * P:(c + 1) * P], xcol[:, par], start=True, stop=True)
                ins.then_inc(h_full, 1)

        def down(j, par):
            pe.wait_ge(h_act, j * 2 + 2)
            need(pe, y_read, j)
            for s in range(HALVES):
                for c in range(FC):
                    ins = pe.matmul(ps_yy[:, s * P:(s + 1) * P], act_h[:, par, c, s * P:(s + 1) * P], w2[:, par, c], start=c == 0, stop=c == FC - 1)
            ins.then_inc(y_full, 1)

        def tile(j, par):
            transposed(j, par)
            up(j, par)
            if not (isinstance(j, int) and j == 0):
                down(j - 1, 1 - par)
        tile(0, 0)
        tile(1, 1)
        tile(2, 0)
        with pe.Fori(1, NJ // 2) as i:
            pair[0] = i
            tile(i * 2 + 1, 1)
            tile(i * 2 + 2, 0)
        down(NJ - 1, 0)

    block.__exit__(None, None, None)


_INS = ['x', 'ctx_1024', 'L0_attn_W_in', 'L0_attn_conv_w', 'L0_attn_conv_b', 'L0_attn_W_x', 'L0_attn_W_dt',
        'L0_attn_b_dt', 'L0_attn_A_log', 'L0_attn_D', 'L0_attn_W_out', 'L0_xattn_Wq', 'L0_xattn_Wk',
        'L0_xattn_Wv', 'L0_xattn_gru_wih', 'L0_xattn_gru_whh', 'L0_xattn_gru_bih', 'L0_xattn_gru_bhh',
        'L0_xattn_slot_norm_w', 'L0_xattn_input_norm_w', 'L0_ffn_Wr', 'L0_ffn_br', 'L0_ffn_W1', 'L0_ffn_W2']


def kernel(**inputs):
    import numpy as np
    import concourse.bacc as bacc
    from concourse import mybir as mb
    from concourse.bass_utils import run_bass_kernel_spmd as run

    nc = bacc.Bacc("TRN2", target_bir_lowering=False, num_devices=1)
    arrays, tensors = {}, {}
    for name in _INS:
        a = np.ascontiguousarray(inputs[name])
        arrays[f"in_{name}"] = a
        tensors[name] = nc.dram_tensor(f"in_{name}", a.shape, mb.dt.from_np(a.dtype), kind="ExternalInput").ap()
    out = nc.dram_tensor("out_x", OUT_SHAPE, F32, kind="ExternalOutput").ap()
    build_program(nc, tensors, out)
    r = run(nc, [arrays], core_ids=[0])
    return r.results[0]["out_x"]


OUT_SHAPE = (64, 128, 128)
```

```python
from contextlib import ExitStack

import concourse.bass as bass
from concourse import mybir

ALU = mybir.AluOpType
ACT = mybir.ActivationFunctionType
F32 = mybir.dt.float32
BF16 = mybir.dt.bfloat16
I32 = mybir.dt.int32
AX_X = mybir.AxisListType.X

P = 128
GB = 4
T = GB * P
HUGE = 1.0e30
LN_EPS = 1e-5
RMS_EPS = 1e-6


def after(count_per_group, k, g):
    return g * count_per_group + (k + 1)


def need(eng, sem, value):
    if isinstance(value, int) and value <= 0:
        return
    eng.wait_ge(sem, value)


def hold(eng, sem, value, passed):
    eng.wait_ge(sem, value)
    eng.sem_inc(passed, 1)


def places(nc, stage):
    def sb(name, shape, dt=F32):
        return stage.enter_context(nc.sbuf_tensor(name, shape, dt))

    def psum(name, shape, dt=F32):
        return stage.enter_context(nc.psum_tensor(name, shape, dt))

    def sem(name):
        return stage.enter_context(nc.semaphore(name))

    return sb, psum, sem


def build_program(nc, t, out):
    x, ctx_in = t["x"], t["ctx_1024"]
    B, L, D = x.shape
    DI = t["L0_attn_D"].shape[0]
    NS = t["L0_attn_A_log"].shape[1]
    R = t["L0_attn_W_dt"].shape[0]
    C = DI // P
    NG = B // GB
    NT = B * L
    assert L == P and D == P and C == 2 and R + 2 * NS == 96 and T == 512 and NG % 2 == 0

    with ExitStack() as stack:
        ident = stack.enter_context(nc.sbuf_tensor("ident", [P, P], F32))
        x2 = stack.enter_context(nc.sbuf_tensor("x2", [P, B, D], F32))
        with ExitStack() as first_two:
            x1T = first_two.enter_context(nc.sbuf_tensor("x1T", [P, NT], F32))
            with ExitStack() as stage:
                mamba_stage(nc, t, *places(nc, stage), x1T, ident, NG, NS, C, R)
            with ExitStack() as stage:
                slot_stage(nc, t, *places(nc, stage), x1T, x2, ident, NG)
        with ExitStack() as stage:
            expert_stage(nc, t, *places(nc, stage), x2, ident, out)


def mamba_stage(nc, t, sb, psum, sem, x1T, ident, NG, NS, C, R):
    KW = t["L0_attn_conv_w"].shape[1]
    U = NS * C
    w_in = sb("w_in", [P, 4 * P])
    conv_row = sb("conv_row", [P, C * P, KW])
    w_conv = sb("w_conv", [P, KW, C * P])
    conv_b = sb("conv_b", [P, C])
    w_dtlow = sb("w_dtlow", [P, C, R])
    w_bc3 = sb("w_bc3", [P, C, 3, 2 * NS])
    w_dt = sb("w_dt", [R, C * P])
    b_dt = sb("b_dt", [P, C])
    a_neg = sb("a_neg", [P, C, NS])
    d_half = sb("d_half", [P, C])
    w_out = sb("w_out", [P, C, P])
    pick = sb("pick", [96, 2 * NS, P], BF16)
    minus_half = sb("minus_half", [P, GB])
    x_tok = sb("x_tok", [P, GB, P])
    x_res = sb("x_res", [P, GB, P])
    xT = sb("xT", [P, GB, KW - 1 + P])
    xc = sb("xc", [P, C, T])
    th = sb("th", [P, C, T])
    thz = sb("thz", [P, C, T])
    zc = sb("zc", [P, C, T])
    bc_raw = sb("bc_raw", [96, T])
    xd = sb("xd", [P, C, T])
    xb2 = sb("xb2", [P, 2, C, T])
    sz2 = sb("sz2", [P, 2, C, T])
    dt_low = sb("dt_low", [R, T])
    bc_split = sb("bc_split", [96, 2, T], BF16)
    bc_rest = sb("bc_rest", [96, T])
    bc_mid = sb("bc_mid", [96, T], BF16)
    sp_abs = sb("sp_abs", [P, C, T])
    sp_relu = sb("sp_relu", [P, C, T])
    dt = sb("dt", [P, 2, C, T])
    dtx = sb("dtx", [P, 2, C, T])
    inp = sb("inp", [P, 4, T])
    state = sb("state", [P, 4, T])
    c_bc = sb("c_bc", [P, 2, T])
    hc = sb("hc", [P, 4, T])
    yd = sb("yd", [P, C, T])
    yz = sb("yz", [P, C, T])
    o_sb = sb("o_sb", [P, T])
    res = sb("res", [P, GB, P])
    stats = sb("stats", [P, GB, 6])
    mv = sb("mv", [P, GB, 2])
    veps = sb("veps", [P, GB])
    rstd = sb("rstd", [P, GB])
    ps_misc = psum("ps_misc", [P, T])
    ps_da = [psum(f"ps_da{i}", [P, T]) for i in range(2)]
    ps_b = [psum(f"ps_b{i}", [P, T]) for i in range(2)]
    ps_c = psum("ps_c", [P, T])
    ps_y = [psum(f"ps_y{c}", [P, T]) for c in range(C)]

    w_loaded = sem("w_loaded")
    consts_pool = sem("consts_pool")
    w_scaled = sem("w_scaled")
    a_ready = sem("a_ready")
    x_loaded = sem("x_loaded")
    res_loaded = sem("res_loaded")
    misc_full = sem("misc_full")
    act_pre = sem("act_pre")
    dve_pre = sem("dve_pre")
    pool_pre = sem("pool_pre")
    da_ready = sem("da_ready")
    b_ready = sem("b_ready")
    c_full = sem("c_full")
    c_ready = sem("c_ready")
    inp_ready = sem("inp_ready")
    state_ready = sem("state_ready")
    hc_ready = sem("hc_ready")
    y_added = sem("y_added")
    y_taken = sem("y_taken")
    yz_ready = sem("yz_ready")
    res_ready = sem("res_ready")
    ln_step = sem("ln_step")
    rstd_ready = sem("rstd_ready")
    x1_ready = sem("x1_ready")
    x1T_ready = sem("x1T_ready")
    pool_passed = sem("pool_passed")
    dve_passed = sem("dve_passed")

    xv = t["x"].rearrange("(g b) l d -> l g b d", b=GB)
    NW = 12

    MISC_PRE = ["xT", "xb0", "xb1", "z0", "z1", "dtlow", "bc", "dt0", "dt1"]
    ACT_PRE = ["xT", "xc0", "xc1", "th0", "zc0", "th1", "zc1", "thz0", "thz1", "dtlow", "raw", "hi",
               "xd0", "xd1", "abs", "exp", "mid_row", "ln"]
    DVE_PRE = ["xb0", "xb1", "z0", "z1", "rest", "low", "relu", "dt", "dtx"]
    POOL_PRE = ["mid", "first"]
    PE_SLOT = {0: "xT", 1: "xb0", 2: "xb1", 3: "z0", 4: "z1", 6: "dtlow", 7: "bc", 8: "dt0", 9: "dt1"}

    def misc(name, g):
        return after(len(MISC_PRE), MISC_PRE.index(name), g)

    def apre(name, g):
        return after(len(ACT_PRE), ACT_PRE.index(name), g)

    def dpre(name, g):
        return after(len(DVE_PRE), DVE_PRE.index(name), g)

    def ppre(name, g):
        return after(len(POOL_PRE), POOL_PRE.index(name), g)

    tail_read = sem("tail_read")
    tail_full = sem("tail_full")

    def over_groups(eng, group):
        group(0, 0, True, False)
        group(1, 1, False, False)
        with eng.Fori(1, NG // 2 - 1) as i:
            group(i * 2, 0, False, False)
            group(i * 2 + 1, 1, False, False)
        group(NG - 2, 0, False, False)
        group(NG - 1, 1, False, True)

    block = nc.Block()
    blk = block.__enter__()

    @blk.sync
    def _(sp):
        for dst, src in [
            (w_in[:], t["L0_attn_W_in"]),
            (conv_row[:].rearrange("p c k -> p (c k)"), t["L0_attn_conv_w"].rearrange("(o c) k -> o (c k)", o=1).broadcast_to([P, C * P * KW])),
            (conv_b[:], t["L0_attn_conv_b"].rearrange("(c p) -> p c", p=P)),
            (w_dtlow[:], t["L0_attn_W_x"][:, 0:R].rearrange("(c p) k -> p c k", p=P)),
            (w_dt[:], t["L0_attn_W_dt"]),
            (b_dt[:], t["L0_attn_b_dt"].rearrange("(c p) -> p c", p=P)),
            (a_neg[:], t["L0_attn_A_log"].rearrange("(c p) n -> p c n", p=P)),
            (d_half[:], t["L0_attn_D"].rearrange("(c p) -> p c", p=P)),
            (w_out[:], t["L0_attn_W_out"].rearrange("(c p) d -> p c d", p=P)),
        ] + [(w_bc3[:, :, j, :], t["L0_attn_W_x"][:, R:].rearrange("(c p) k -> p c k", p=P)) for j in range(3)]:
            sp.dma_start(dst, src, allow_slow_non_contiguous=True).then_inc(w_loaded, 16)
        sp.dma_start(x_tok[:], xv[:, 0]).then_inc(x_loaded, 16)

        def group(g, par, first, last):
            if not last:
                sp.wait_ge(misc_full, misc("xT", g))
                sp.dma_start(x_tok[:], xv[:, bass.ds(g + 1, 1)].rearrange("l g b d -> l (g b) d")).then_inc(x_loaded, 16)
            if not first:
                sp.wait_ge(res_ready, g)
            sp.dma_start(x_res[:], xv[:, bass.ds(g, 1)].rearrange("l g b d -> l (g b) d")).then_inc(res_loaded, 16)
        over_groups(sp, group)

    @blk.gpsimd
    def _(pool):
        pool.memset(ident[:], 0.0).then_inc(consts_pool, 1)
        pool.memset(pick[:], 0.0).then_inc(consts_pool, 1)
        pool.memset(minus_half[:], -0.5).then_inc(consts_pool, 1)
        pool.memset(xT[:], 0.0).then_inc(consts_pool, 1)
        pool.wait_ge(consts_pool, 4)
        pool.affine_select(out=ident[:], in_=ident[:], compare_op=ALU.not_equal, fill=1.0, base=0,
                           pattern=[[-1, P]], channel_multiplier=1).then_inc(consts_pool, 1)
        for j in range(3):
            pool.affine_select(out=pick[:], in_=pick[:], compare_op=ALU.not_equal, fill=1.0, base=-32 * j,
                               pattern=[[-1, 2 * NS], [0, P]], channel_multiplier=1).then_inc(consts_pool, 1)
            pool.wait_ge(consts_pool, 6 + j)

        def split_mid(g, par):
            hold(pool, dve_pre, dpre("rest", g), pool_passed)
            pool.tensor_copy(bc_mid[:], bc_rest[:]).then_inc(pool_pre, 1)

        def first_steps(g, par):
            hold(pool, dve_pre, dpre("dtx", g), pool_passed)
            pool.memset(dt[:, par].rearrange("p c (b l) -> p (c b) l", l=P)[:, :, 0:1], HUGE).then_inc(pool_pre, 1)

        def gated(g, par):
            need(pool, tail_full, after(2, 0, g - 1))
            for c in range(C):
                pool.wait_ge(y_taken, after(C, c, g))
                pool.tensor_tensor(yz[:, c], yd[:, c], sz2[:, par, c], ALU.mult).then_inc(yz_ready, 1)

        split_mid(0, 0)
        first_steps(0, 0)

        def group(g, par, first, last):
            for n in range(NS):
                for c in range(C):
                    u = n * C + c
                    pool.wait_ge(state_ready, after(U, u, g))
                    if c == 0:
                        pool.wait_ge(c_ready, after(NS, n, g))
                    need(pool, y_added, after(U, u, g) - 4)
                    pool.tensor_tensor(hc[:, u % 4], state[:, u % 4], c_bc[:, n % 2], ALU.mult).then_inc(hc_ready, 1)
                if not last:
                    if n == 9:
                        split_mid(g + 1, 1 - par)
                    if n == 14:
                        first_steps(g + 1, 1 - par)
                if not first and n == 2:
                    gated(g - 1, 1 - par)
                if not first and n == 9:
                    pool.wait_ge(ln_step, after(3, 2, g - 1))
                    pool.tensor_tensor(rstd[:], veps[:], minus_half[:], ALU.pow).then_inc(rstd_ready, 1)
        over_groups(pool, group)
        gated(NG - 1, 1)
        pool.wait_ge(ln_step, after(3, 2, NG - 1))
        pool.tensor_tensor(rstd[:], veps[:], minus_half[:], ALU.pow).then_inc(rstd_ready, 1)

    @blk.scalar
    def _(act):
        act.wait_ge(w_loaded, 16 * NW)
        act.activation(a_neg[:], a_neg[:], ACT.Exp).then_inc(a_ready, 1)
        act.wait_ge(a_ready, 1)
        act.mul(a_neg[:], a_neg[:], -1.0).then_inc(a_ready, 1)
        act.wait_ge(a_ready, 2)
        act.wait_ge(w_scaled, 4 + KW)
        act.wait_ge(consts_pool, 8)

        def evacuate(g, par, name):
            act.wait_ge(misc_full, misc(name, g))
            if name == "xT":
                act.copy(xT[:, :, KW - 1:], ps_misc[:].rearrange("p (b l) -> p b l", l=P)).then_inc(act_pre, 1)
            if name in ("xb0", "xb1"):
                c = int(name[2])
                need(act, dve_pre, dpre(f"xb{c}", g - 1))
                act.activation(xc[:, c], ps_misc[:], ACT.Identity, bias=conv_b[:, c:c + 1]).then_inc(act_pre, 1)
            if name in ("z0", "z1"):
                c = int(name[1])
                need(act, dve_pre, dpre(f"z{c}", g - 1))
                act.copy(zc[:, c], ps_misc[:]).then_inc(act_pre, 1)
            if name == "dtlow":
                act.copy(dt_low[:], ps_misc[0:R]).then_inc(act_pre, 1)
            if name == "bc":
                need(act, dve_pre, dpre("rest", g - 1))
                act.copy(bc_raw[:], ps_misc[0:96]).then_inc(act_pre, 1)
                act.copy(bc_split[:, par], ps_misc[0:96]).then_inc(act_pre, 1)
            if name in ("dt0", "dt1"):
                c = int(name[2])
                need(act, dve_pre, dpre("relu", g - 1))
                act.activation(xd[:, c], ps_misc[:], ACT.Identity, bias=b_dt[:, c:c + 1]).then_inc(act_pre, 1)

        def piece_th(g, c):
            act.wait_ge(act_pre, apre(f"xc{c}", g))
            act.activation(th[:, c], xc[:, c], ACT.Tanh, scale=0.5).then_inc(act_pre, 1)

        def piece_thz(g, c):
            act.wait_ge(act_pre, apre(f"zc{c}", g))
            act.activation(thz[:, c], zc[:, c], ACT.Tanh, scale=0.5).then_inc(act_pre, 1)

        def piece_abs(g):
            act.wait_ge(act_pre, apre("xd1", g))
            need(act, dve_pre, dpre("dt", g - 1))
            act.activation(sp_abs[:], xd[:], ACT.Abs).then_inc(act_pre, 1)
            act.wait_ge(act_pre, apre("abs", g))
            act.activation(sp_abs[:], sp_abs[:], ACT.Exp, scale=-1.0).then_inc(act_pre, 1)

        def piece_ln(g, par):
            act.wait_ge(pool_pre, ppre("mid", g))
            act.copy(bc_split[32:64, par], bc_mid[32:64]).then_inc(act_pre, 1)
            act.wait_ge(act_pre, apre("exp", g))
            act.activation(sp_abs[:], sp_abs[:], ACT.Ln, bias=1.0).then_inc(act_pre, 1)

        def prepare(g, par, n):
            if n in (3, 4):
                piece_th(g, n - 3)
            if n in (5, 6):
                piece_thz(g, n - 5)
            if n == 11:
                piece_abs(g)
            if n == 12:
                piece_ln(g, par)

        def decay(g, par, n, c):
            u = n * C + c
            if u == 0:
                act.wait_ge(pool_pre, ppre("first", g))
            need(act, state_ready, after(U, u, g) - 2)
            act.activation(ps_da[u % 2][:], dt[:, par, c], ACT.Exp, scale=a_neg[:, c, n:n + 1]).then_inc(da_ready, 1)

        def copy_c(g, par, n):
            act.wait_ge(c_full, after(NS, n, g))
            need(act, hc_ready, after(U, n * C + 1, g) - 4)
            act.copy(c_bc[:, n % 2], ps_c[:]).then_inc(c_ready, 1)

        def finish(g):
            act.wait_ge(tail_full, after(2, 1, g))
            act.copy(x1T[:, bass.ds(g * T, T)], ps_misc[:]).then_inc(x1T_ready, 1)

        def copy_o(g):
            act.wait_ge(tail_full, after(2, 0, g))
            need(act, res_ready, g)
            act.copy(o_sb[:], ps_misc[:]).then_inc(tail_read, 1)

        for n in range(NS):
            if n - 1 in PE_SLOT:
                evacuate(0, 0, PE_SLOT[n - 1])
            prepare(0, 0, n)
        copy_c(0, 0, 0)
        decay(0, 0, 0, 0)
        decay(0, 0, 0, 1)

        def group(g, par, first, last):
            for n in range(NS):
                if n < NS - 1:
                    copy_c(g, par, n + 1)
                if not last and n - 1 in PE_SLOT:
                    evacuate(g + 1, 1 - par, PE_SLOT[n - 1])
                if not first and n == 6:
                    copy_o(g - 1)
                if not first and n == 13:
                    finish(g - 1)
                if n < NS - 1:
                    decay(g, par, n + 1, 0)
                if not last:
                    prepare(g + 1, 1 - par, n)
                if n < NS - 1:
                    decay(g, par, n + 1, 1)
            if not last:
                copy_c(g + 1, 1 - par, 0)
                decay(g + 1, 1 - par, 0, 0)
                decay(g + 1, 1 - par, 0, 1)
        over_groups(act, group)
        copy_o(NG - 1)
        finish(NG - 1)

    @blk.vector
    def _(dve):
        dve.wait_ge(w_loaded, 16 * NW)
        dve.tensor_scalar_mul(w_dtlow[:], w_dtlow[:], 0.5).then_inc(w_scaled, 1)
        dve.tensor_scalar_mul(w_bc3[:], w_bc3[:], 0.5).then_inc(w_scaled, 1)
        dve.tensor_scalar_mul(d_half[:], d_half[:], 0.5).then_inc(w_scaled, 1)
        dve.tensor_scalar_mul(w_out[:], w_out[:], 0.5).then_inc(w_scaled, 1)
        for k in range(KW):
            dve.tensor_tensor(w_conv[:, k], w_in[:, 0:C * P], conv_row[:, :, k], ALU.mult).then_inc(w_scaled, 1)
        dve.wait_ge(w_scaled, 4 + KW)

        def silus(g, par, c):
            dve.wait_ge(act_pre, apre(f"th{c}", g))
            need(dve, y_taken, after(C, C - 1, g - 2))
            dve.scalar_tensor_tensor(xb2[:, par, c], th[:, c], 1.0, xc[:, c], ALU.add, ALU.mult).then_inc(dve_pre, 1)

        def zsilu(g, par, c):
            dve.wait_ge(act_pre, apre(f"thz{c}", g))
            need(dve, yz_ready, after(C, C - 1, g - 2))
            dve.scalar_tensor_tensor(sz2[:, par, c], thz[:, c], 1.0, zc[:, c], ALU.add, ALU.mult).then_inc(dve_pre, 1)

        def rest(g, par):
            dve.wait_ge(act_pre, apre("hi", g))
            need(dve, pool_pre, ppre("mid", g - 1))
            dve.tensor_tensor(bc_rest[:], bc_raw[:], bc_split[:, par], ALU.subtract).then_inc(dve_pre, 1)

        def low(g, par):
            dve.wait_ge(pool_pre, ppre("mid", g))
            dve.tensor_tensor(bc_split[64:96, par], bc_rest[64:96], bc_mid[64:96], ALU.subtract).then_inc(dve_pre, 1)

        def relu(g):
            dve.wait_ge(act_pre, apre("xd1", g))
            dve.tensor_scalar_max(sp_relu[:], xd[:], 0.0).then_inc(dve_pre, 1)

        def dts(g, par):
            dve.wait_ge(act_pre, apre("ln", g))
            dve.wait_ge(dve_pre, dpre("relu", g))
            dve.tensor_tensor(dt[:, par], sp_relu[:], sp_abs[:], ALU.add).then_inc(dve_pre, 1)

        def dtxs(g, par):
            dve.wait_ge(dve_pre, dpre("dt", g))
            dve.scalar_tensor_tensor(dtx[:, par], dt[:, par], 0.5, xb2[:, par], ALU.mult, ALU.mult).then_inc(dve_pre, 1)

        def prepare(g, par, n):
            if n in (4, 5):
                silus(g, par, n - 4)
            if n in (6, 7):
                zsilu(g, par, n - 6)
            if n == 9:
                rest(g, par)
            if n == 10:
                low(g, par)
            if n == 11:
                relu(g)
            if n == 13:
                dts(g, par)
            if n == 14:
                dtxs(g, par)

        def tail(g, par, n):
            if n == 1:
                dve.wait_ge(y_added, after(U, U - 1, g))
                need(dve, yz_ready, after(C, C - 1, g - 1))
                for c in range(C):
                    dve.scalar_tensor_tensor(yd[:, c], xb2[:, par, c], d_half[:, c:c + 1], ps_y[c][:], ALU.mult, ALU.add).then_inc(y_taken, 1)
            if n == 7:
                dve.wait_ge(tail_read, after(1, 0, g))
                dve.wait_ge(res_loaded, 16 * g + 16)
                dve.tensor_tensor(res[:], o_sb[:].rearrange("p (b d) -> p b d", d=P), x_res[:], ALU.add).then_inc(res_ready, 1)
            if n == 8:
                dve.wait_ge(res_ready, after(1, 0, g))
                for b in range(GB):
                    ins = dve.bn_stats(stats[:, b], res[:, b])
                ins.then_inc(ln_step, 1)
                hold(dve, ln_step, after(3, 0, g), dve_passed)
                for b in range(GB):
                    ins = dve.bn_aggr(mv[:, b], stats[:, b])
                ins.then_inc(ln_step, 1)
                dve.wait_ge(ln_step, after(3, 1, g))
                dve.tensor_scalar_add(veps[:], mv[:, :, 1], LN_EPS).then_inc(ln_step, 1)
            if n == 10:
                dve.wait_ge(rstd_ready, after(1, 0, g))
                for b in range(GB):
                    ins = dve.tensor_scalar(res[:, b], res[:, b], mv[:, b, 0:1], rstd[:, b:b + 1], ALU.subtract, ALU.mult)
                ins.then_inc(x1_ready, 1)

        def feed(g, par, n, c):
            u = n * C + c
            if u == 0:
                dve.wait_ge(dve_pre, dpre("dtx", g))
            if c == 0:
                dve.wait_ge(b_ready, after(NS, n, g))
            need(dve, state_ready, after(U, u, g) - 4)
            dve.tensor_tensor(inp[:, u % 4], dtx[:, par, c], ps_b[n % 2][:], ALU.mult).then_inc(inp_ready, 1)

        def scan(g, par, n, c):
            u = n * C + c
            dve.wait_ge(da_ready, after(U, u, g))
            dve.wait_ge(inp_ready, after(U, u, g))
            need(dve, hc_ready, after(U, u, g) - 4)
            dve.tensor_tensor_scan(state[:, u % 4], ps_da[u % 2][:], inp[:, u % 4], 0.0, ALU.mult, ALU.add).then_inc(state_ready, 1)

        for n in range(NS):
            prepare(0, 0, n)
        feed(0, 0, 0, 0)

        def group(g, par, first, last):
            for n in range(NS):
                feed(g, par, n, 1)
                scan(g, par, n, 0)
                if not last:
                    prepare(g + 1, 1 - par, n)
                if n < NS - 1:
                    feed(g, par, n + 1, 0)
                elif not last:
                    feed(g + 1, 1 - par, 0, 0)
                scan(g, par, n, 1)
                if not first:
                    tail(g - 1, 1 - par, n)
        over_groups(dve, group)
        for n in range(NS):
            tail(NG - 1, 1, n)

    @blk.tensor
    def _(pe):
        pe.wait_ge(w_loaded, 16 * NW)
        pe.wait_ge(w_scaled, 4 + KW)
        pe.wait_ge(consts_pool, 8)

        def fill_misc(g, par, name):
            if name == "xT":
                pe.wait_ge(x_loaded, 16 * g + 16)
                need(pe, act_pre, apre("xd1", g - 1))
                need(pe, x1T_ready, g - 2)
                for b in range(GB):
                    ins = pe.transpose(ps_misc[:, b * P:(b + 1) * P], x_tok[:, b], ident[:])
            if name in ("xb0", "xb1"):
                c = int(name[2])
                pe.wait_ge(act_pre, apre(("xT", "xc0")[c], g))
                for k in range(KW):
                    ins = pe.matmul(ps_misc[:].rearrange("p (b l) -> p b l", l=P), w_conv[:, k, c * P:(c + 1) * P], xT[:, :, k:k + P], start=k == 0, stop=k == KW - 1)
            if name in ("z0", "z1"):
                c = int(name[1])
                pe.wait_ge(act_pre, apre(("xc1", "zc0")[c], g))
                ins = pe.matmul(ps_misc[:].rearrange("p (b l) -> p b l", l=P), w_in[:, (C + c) * P:(C + c + 1) * P], xT[:, :, KW - 1:], start=True, stop=True)
            if name == "dtlow":
                pe.wait_ge(act_pre, apre("zc1", g))
                need(pe, tail_read, g - 1)
                pe.wait_ge(dve_pre, dpre("xb1", g))
                for c in range(C):
                    ins = pe.matmul(ps_misc[0:R], w_dtlow[:, c], xb2[:, par, c], start=c == 0, stop=c == C - 1)
            if name == "bc":
                pe.wait_ge(act_pre, apre("dtlow", g))
                for c in range(C):
                    ins = pe.matmul(ps_misc[0:96], w_bc3[:, c].rearrange("p j k -> p (j k)"), xb2[:, par, c], start=c == 0, stop=c == C - 1)
            if name in ("dt0", "dt1"):
                c = int(name[2])
                pe.wait_ge(act_pre, apre(("hi", "xd0")[c], g))
                ins = pe.matmul(ps_misc[:], w_dt[:, c * P:(c + 1) * P], dt_low[:], start=True, stop=True)
            ins.then_inc(misc_full, 1)

        def tail(g, n):
            if n == 5:
                pe.wait_ge(yz_ready, after(C, C - 1, g))
                for b in range(GB):
                    for c in range(C):
                        ins = pe.matmul(ps_misc[:, b * P:(b + 1) * P], yz[:, c, b * P:(b + 1) * P], w_out[:, c], start=c == 0, stop=c == C - 1)
                ins.then_inc(tail_full, 1)
            if n == 12:
                pe.wait_ge(x1_ready, after(1, 0, g))
                for b in range(GB):
                    ins = pe.transpose(ps_misc[:, b * P:(b + 1) * P], res[:, b], ident[:])
                ins.then_inc(tail_full, 1)

        def spread(g, par, n):
            if n == 0:
                pe.wait_ge(act_pre, apre("mid_row", g))
                pe.wait_ge(dve_pre, dpre("low", g))
            need(pe, inp_ready, after(U, n * C + 1, g) - 4)
            pe.matmul(ps_b[n % 2][:], pick[:, n], bc_split[:, par], start=True, stop=True).then_inc(b_ready, 1)
            need(pe, c_ready, after(NS, n, g) - 1)
            pe.matmul(ps_c[:], pick[:, NS + n], bc_split[:, par], start=True, stop=True).then_inc(c_full, 1)

        def add_y(g, n):
            for c in range(C):
                u = n * C + c
                pe.wait_ge(hc_ready, after(U, u, g))
                if n == 0:
                    need(pe, y_taken, after(C, c, g - 1))
                pe.matmul(ps_y[c][:], ident[:], hc[:, u % 4], start=n == 0, stop=n == NS - 1).then_inc(y_added, 1)

        for n in range(NS):
            if n in PE_SLOT:
                fill_misc(0, 0, PE_SLOT[n])
        spread(0, 0, 0)

        def group(g, par, first, last):
            for n in range(NS):
                if n < NS - 1:
                    spread(g, par, n + 1)
                elif not last:
                    spread(g + 1, 1 - par, 0)
                if n == 0 and not first:
                    add_y(g - 1, NS - 1)
                if n > 0:
                    add_y(g, n - 1)
                if not last and n in PE_SLOT:
                    fill_misc(g + 1, 1 - par, PE_SLOT[n])
                if not first and n == 5:
                    if last:
                        need(pe, x1T_ready, g - 1)
                    else:
                        pe.wait_ge(act_pre, apre("zc1", g + 1))
                if not first and n == 12 and not last:
                    pe.wait_ge(act_pre, apre("xd1", g + 1))
                if not first:
                    tail(g - 1, n)
        over_groups(pe, group)
        add_y(NG - 1, NS - 1)
        pe.wait_ge(x1T_ready, NG - 1)
        tail(NG - 1, 5)
        tail(NG - 1, 12)

    block.__exit__(None, None, None)


ITERS = 3


def slot_stage(nc, t, sb, psum, sem, x1T, x2, ident, NG):
    M = t["ctx_1024"].shape[1]
    NQ = NG // 2
    SCALE = float(P) ** -0.5
    ctx = sb("ctx", [M, 2, GB, P])
    ctx_sq = sb("ctx_sq", [M, P])
    ctx_ss = sb("ctx_ss", [M, 2, GB])
    ctx_r = sb("ctx_r", [M, 2, GB])
    pn = sb("pn", [M, 2, GB, P])
    pnT = sb("pnT", [P, GB * M])
    kq = sb("kq", [P, 2, 2, GB * M])
    vw = sb("vw", [M, 2, 2, GB, 3 * P])
    wq = sb("wq", [P, P])
    wk = sb("wk", [P, P])
    wv = sb("wv", [P, P])
    wih = sb("wih", [P, 3, P])
    whh = sb("whh", [P, 3, P])
    w_slot = sb("w_slot", [P, 1])
    w_input = sb("w_input", [P, 1])
    bih = sb("bih", [P, 3])
    bhh = sb("bhh", [P, 3])
    bias = sb("bias", [P, 3])
    wihT = sb("wihT", [P, 3 * P])
    whhT = sb("whhT", [P, 3 * P])
    kq_w = sb("kq_w", [P, P])
    vw_w = sb("vw_w", [P, 3 * P])
    ones = sb("ones", [P, P])
    m_half = sb("m_half", [P, GB])
    h = [[sb(f"h{par}{k}", [P, T]) for k in range(2)] for par in range(2)]
    sq = [sb(f"sq{k}", [P, T]) for k in range(2)]
    sn = [sb(f"sn{k}", [P, T]) for k in range(2)]
    ms = [sb(f"ms{k}", [P, GB]) for k in range(2)]
    rs = [sb(f"rs{k}", [P, GB]) for k in range(2)]
    mx = [sb(f"mx{k}", [M, GB]) for k in range(2)]
    nmx = [sb(f"nmx{k}", [M, GB]) for k in range(2)]
    ex = [sb(f"ex{k}", [M, T]) for k in range(2)]
    se = [sb(f"se{k}", [M, GB]) for k in range(2)]
    rse = [sb(f"rse{k}", [M, GB]) for k in range(2)]
    dn = [sb(f"dn{k}", [P, GB]) for k in range(2)]
    rdn = [sb(f"rdn{k}", [P, GB]) for k in range(2)]
    at = [sb(f"at{k}", [M, T]) for k in range(2)]
    hnb = sb("hnb", [P, T])
    tr = sb("tr", [P, T])
    tz = sb("tz", [P, T])
    nn = sb("nn", [P, T])
    rh = sb("rh", [P, T])
    pre = sb("pre", [P, T])
    df = sb("df", [P, T])
    zd = sb("zd", [P, T])
    res2 = [sb(f"res2_{k}", [P, T]) for k in range(2)]
    tok = [sb(f"tok{k}", [P, GB, P]) for k in range(2)]
    stats2 = [sb(f"stats2_{k}", [P, GB, 6]) for k in range(2)]
    mv2 = [sb(f"mv2_{k}", [P, GB, 2]) for k in range(2)]
    veps2 = [sb(f"veps2_{k}", [P, GB]) for k in range(2)]
    rstd2 = [sb(f"rstd2_{k}", [P, GB]) for k in range(2)]
    ps_s = [psum(f"ps_s{k}", [P, T]) for k in range(2)]
    ps_r = psum("ps_r", [P, T])
    ps_z = psum("ps_z", [P, T])
    ps_hn = psum("ps_hn", [P, T])
    ps_xn = psum("ps_xn", [P, T])
    ps_u = [psum(f"ps_u{k}", [P, T]) for k in range(2)]

    PE1 = ["ssq", "rbc", "scores", "den", "dbc"]
    PE2 = ["hn", "r", "xn", "z"]
    V = ["ms", "sn", "mx", "nmx", "rse", "dn", "rdn", "attn"]
    V2 = ["rh", "pre", "df", "zd", "h"]
    A2 = ["hnb", "tr", "nn", "tz"]
    U_SEQ = ["tp0", "P0", "K0", "tp1", "v00", "v01", "v02", "v03", "P1", "K1", "v10", "v11", "v12", "v13"]
    U_PLACE = {(0, 0): ["tp0", "P0"], (0, 1): ["K0"], (1, 0): ["tp1", "v00"], (1, 1): ["v01"],
               (2, 0): ["v02"], (2, 1): ["v03"], (3, 0): ["P1"], (3, 1): ["K1"],
               (4, 0): ["v10"], (4, 1): ["v11"], (5, 0): ["v12"], (5, 1): ["v13"]}
    CONTEXT = [u for u in U_SEQ if u[0] != "t"]
    POSTV = ["res2", "stats", "aggr", "veps", "x2"]
    loaded = sem("slot_w_loaded")
    const2 = sem("const2")
    prep_pe = sem("prep_pe")
    prep_act = sem("prep_act")
    prep_v = sem("prep_v")
    pe1 = [sem(f"pe1_{k}") for k in range(2)]
    pe2 = [sem(f"pe2_{k}") for k in range(2)]
    dve1 = [sem(f"dve1_{k}") for k in range(2)]
    dve2 = [sem(f"dve2_{k}") for k in range(2)]
    squared = [sem(f"squared{k}") for k in range(2)]
    exped = [sem(f"exped{k}") for k in range(2)]
    act2 = [sem(f"act2_{k}") for k in range(2)]
    rooted = [sem(f"rooted{k}") for k in range(2)]
    h_loaded = [sem(f"h_loaded{k}") for k in range(2)]
    post_v = [sem(f"post_v{k}") for k in range(2)]
    post_root = [sem(f"post_root{k}") for k in range(2)]
    ctx_loaded = [sem(f"ctx_loaded{k}") for k in range(2)]
    ctx_sumsq = [sem(f"ctx_sumsq{k}") for k in range(2)]
    ctx_ms = [sem(f"ctx_ms{k}") for k in range(2)]
    ctx_root = [sem(f"ctx_root{k}") for k in range(2)]
    ctx_normed = [sem(f"ctx_normed{k}") for k in range(2)]
    u_full = sem("u_full")
    u_read = sem("u_read")
    passed2 = [sem(f"passed2_{k}") for k in range(2)]

    def ev(names, name, it):
        return after(len(names), names.index(name), it)

    def u_value(i, name):
        n = len(CONTEXT)
        if isinstance(i, int) and i < 0:
            return CONTEXT.index(name) + 1
        if isinstance(i, int) and i == 0:
            return n + CONTEXT.index(name) + 1
        if isinstance(i, int) and i >= NQ - 1:
            return 2 * n + len(U_SEQ) * (NQ - 2) + 2 * (i - NQ + 1) + int(name[2]) + 1
        return 2 * n + len(U_SEQ) * (i - 1) + U_SEQ.index(name) + 1

    def u_read_tp(lane, q):
        return 0 if isinstance(q, int) and q < 0 else u_value(q + 1, f"tp{lane}")

    def u_names(beat, place, first, last):
        for name in U_PLACE[beat, place]:
            if (not first) if name[0] == "t" else (not last):
                yield name

    def over_pairs(eng, body):
        body(0, 0, True, False)
        body(1, 1, False, False)
        with eng.Fori(1, NQ // 2 - 1) as i:
            body(i * 2, 0, False, False)
            body(i * 2 + 1, 1, False, False)
        body(NQ - 2, 0, False, False)
        body(NQ - 1, 1, False, True)

    def beats(i, par):
        for beat in range(2 * ITERS):
            lane, j = beat % 2, beat // 2
            att = (lane, i * ITERS + j, j, i, par)
            k = j - (1 - lane)
            if k >= 0:
                yield beat, att, (1 - lane, i * ITERS + k, k, i, par)
            else:
                yield beat, att, (1, i * ITERS - 1, ITERS - 1, i - 1, 1 - par)

    block = nc.Block()
    blk = block.__enter__()
    cview = t["ctx_1024"].rearrange("(q k b) m d -> m q k b d", k=2, b=GB)

    def ctx_of(q, k):
        return cview[:, bass.ds(q, 1), k].rearrange("m q b d -> m (q b) d")

    @blk.sync
    def _(sp):
        for dst, src in [
            (wq[:], t["L0_xattn_Wq"]), (wk[:], t["L0_xattn_Wk"]), (wv[:], t["L0_xattn_Wv"]),
            (wih[:], t["L0_xattn_gru_wih"].rearrange("(j p) d -> p j d", p=P)),
            (whh[:], t["L0_xattn_gru_whh"].rearrange("(j p) d -> p j d", p=P)),
            (w_slot[:], t["L0_xattn_slot_norm_w"].rearrange("(p o) -> p o", o=1)),
            (w_input[:], t["L0_xattn_input_norm_w"].rearrange("(p o) -> p o", o=1)),
            (bih[:], t["L0_xattn_gru_bih"].rearrange("(j p) -> p j", p=P)),
            (bhh[:], t["L0_xattn_gru_bhh"].rearrange("(j p) -> p j", p=P)),
        ]:
            sp.dma_start(dst, src, allow_slow_non_contiguous=True).then_inc(loaded, 16)
        for k in range(2):
            sp.dma_start(ctx[:, k], ctx_of(0, k)).then_inc(ctx_loaded[k], 16)
        for k in range(2):
            sp.wait_ge(ctx_normed[k], 1)
            sp.dma_start(ctx[:, k], ctx_of(1, k)).then_inc(ctx_loaded[k], 16)
        with sp.Fori(2, NQ) as q:
            for k in range(2):
                sp.wait_ge(ctx_normed[k], q)
                sp.dma_start(ctx[:, k], ctx_of(q, k)).then_inc(ctx_loaded[k], 16)

    @blk.gpsimd
    def _(pool):
        pool.memset(ones[:], 1.0).then_inc(const2, 1)
        pool.memset(m_half[:], -0.5).then_inc(const2, 1)
        pool.wait_ge(const2, 2)

        def norm_ctx(q, k):
            pool.wait_ge(ctx_ms[k], q + 1)
            pool.tensor_tensor(ctx_r[:, k], ctx_ss[:, k], m_half[0:M], ALU.pow).then_inc(ctx_root[k], 1)
            pool.wait_ge(ctx_root[k], q + 1)
            if not (isinstance(q, int) and q == 0):
                pool.wait_ge(u_full, u_value(q - 2, f"P{k}"))
            pool.tensor_tensor(pn[:, k], ctx[:, k], ctx_r[:, k].rearrange("m (b o) -> m b o", o=1).broadcast_to([M, GB, P]), ALU.mult).then_inc(ctx_normed[k], 1)

        def root(lane, it):
            pool.wait_ge(dve1[lane], ev(V, "ms", it))
            pool.tensor_tensor(rs[lane][:], ms[lane][:], m_half[:], ALU.pow).then_inc(rooted[lane], 1)

        def post_rooting(lane, q):
            pool.wait_ge(post_v[lane], ev(POSTV, "veps", q))
            pool.tensor_tensor(rstd2[lane][:], veps2[lane][:], m_half[:], ALU.pow).then_inc(post_root[lane], 1)

        norm_ctx(0, 0)
        norm_ctx(0, 1)
        norm_ctx(1, 0)

        def body(i, par, first, last):
            for beat, (a, it, j, q, _), _ in beats(i, par):
                root(a, it)
                if beat in (1, 2) and not first:
                    post_rooting(beat - 1, i - 1)
                if beat == 2 and not last:
                    norm_ctx(i + 1, 1)
                if beat == 5 and not last and not (isinstance(i, int) and i == NQ - 2):
                    norm_ctx(i + 2, 0)
        over_pairs(pool, body)
        post_rooting(0, NQ - 1)
        post_rooting(1, NQ - 1)

    @blk.scalar
    def _(act):
        act.wait_ge(loaded, 16 * 9)
        for j in range(2):
            act.wait_ge(prep_pe, j + 1)
            act.copy((wihT, whhT)[j][:], ps_u[j][:, 0:3 * P]).then_inc(prep_act, 1)
        act.wait_ge(prep_pe, 3)
        act.activation(kq_w[:], ps_u[0][:, 0:P], ACT.Copy, scale=w_input[:, 0:1]).then_inc(prep_act, 1)
        act.wait_ge(prep_pe, 4)
        act.activation(vw_w[:], ps_u[1][:, 0:3 * P], ACT.Copy, scale=w_input[:, 0:1]).then_inc(prep_act, 1)
        act.wait_ge(prep_v, 4)

        def sum_ctx(q, k, before):
            act.wait_ge(ctx_loaded[k], 16 * q + 16)
            need(act, ctx_normed[k], q)
            for b in range(GB):
                if b:
                    act.wait_ge(ctx_sumsq[k], q * GB + b)
                elif before is not None:
                    act.wait_ge(ctx_sumsq[before[1]], (before[0] + 1) * GB)
                act.activation(ctx_sq[:], ctx[:, k, b], ACT.Square, accum_out=ctx_ss[:, k, b:b + 1]).then_inc(ctx_sumsq[k], 1)

        def load_h(lane, q, par):
            if not (isinstance(q, int) and q < 2):
                act.wait_ge(post_v[lane], ev(POSTV, "res2", q - 2))
            g = q * 2 + lane
            act.copy(h[par][lane][:], x1T[:, bass.ds(g * T, T)]).then_inc(h_loaded[lane], 1)

        def read_u(i, par, name):
            act.wait_ge(u_full, u_value(i, name))
            lane = int(name[1] if name[0] != "t" else name[2])
            if name[0] == "P":
                act.copy(pnT[:], ps_u[0][:, 0:GB * M]).then_inc(u_read, 1)
            elif name[0] == "K":
                act.activation(kq[:, 1 - par, lane], ps_u[1][:, 0:GB * M], ACT.Copy, scale=w_slot[:, 0:1]).then_inc(u_read, 1)
            elif name[0] == "v":
                b = int(name[2])
                act.copy(vw[:, 1 - par, lane, b], ps_u[b % 2][0:M, 0:3 * P]).then_inc(u_read, 1)
            else:
                need(act, post_v[lane], ev(POSTV, "x2", i - 2))
                act.copy(tok[lane][:].rearrange("p b d -> p (b d)"), ps_u[1][:]).then_inc(u_read, 1)

        def attention_sq(lane, it, j, q, par):
            if j == 0:
                act.wait_ge(h_loaded[lane], q + 1)
            else:
                act.wait_ge(dve2[lane], ev(V2, "h", it - 1))
            act.activation(sq[lane][:], h[par][lane][:], ACT.Square).then_inc(squared[lane], 1)

        def attention_exp(lane, it):
            act.wait_ge(dve1[lane], ev(V, "nmx", it))
            for b in range(GB):
                act.activation(ex[lane][:, b * P:(b + 1) * P], ps_s[lane][0:M, b * P:(b + 1) * P], ACT.Exp,
                               bias=nmx[lane][:, b:b + 1], accum_out=se[lane][:, b:b + 1]).then_inc(exped[lane], 1)

        def gru_before(lane, it):
            return it if lane == 1 else it - 1

        def gru_h(lane, it):
            act.wait_ge(pe2[lane], ev(PE2, "hn", it))
            need(act, dve2[1 - lane], ev(V2, "rh", gru_before(lane, it)))
            act.activation(hnb[:], ps_hn[:], ACT.Identity, bias=bias[:, 2:3], scale=0.5).then_inc(act2[lane], 1)

        def gru_r(lane, it):
            act.wait_ge(pe2[lane], ev(PE2, "r", it))
            act.activation(tr[:], ps_r[:], ACT.Tanh, bias=bias[:, 0:1], scale=0.5).then_inc(act2[lane], 1)

        def gru_nz(lane, it):
            act.wait_ge(dve2[lane], ev(V2, "pre", it))
            need(act, dve2[1 - lane], ev(V2, "h", gru_before(lane, it)))
            act.activation(nn[:], pre[:], ACT.Tanh, bias=bih[:, 2:3]).then_inc(act2[lane], 1)
            act.wait_ge(pe2[lane], ev(PE2, "z", it))
            act.activation(tz[:], ps_z[:], ACT.Tanh, bias=bias[:, 1:2], scale=0.5).then_inc(act2[lane], 1)

        sum_ctx(0, 0, None)
        sum_ctx(0, 1, (0, 0))
        sum_ctx(1, 0, (0, 1))
        for name in CONTEXT:
            read_u(-1, 1, name)
        load_h(0, 0, 0)
        load_h(1, 0, 0)

        def body(i, par, first, last):
            for beat, (a, it, j, q, _), (b, it2, j2, q2, par2) in beats(i, par):
                working = not (first and beat == 0)
                attention_sq(a, it, j, q, par)
                if working:
                    gru_r(b, it2)
                    gru_nz(b, it2)
                for name in u_names(beat, 0, first, last):
                    read_u(i, par, name)
                attention_exp(a, it)
                gru_h(a, it)
                for name in u_names(beat, 1, first, last):
                    read_u(i, par, name)
                if beat == 2 and not last:
                    sum_ctx(i + 1, 1, (i + 1, 0))
                if beat == 3 and not last:
                    load_h(0, i + 1, 1 - par)
                if beat == 4 and not last:
                    load_h(1, i + 1, 1 - par)
                if beat == 5 and not last and not (isinstance(i, int) and i == NQ - 2):
                    sum_ctx(i + 2, 0, (i + 1, 1))
        over_pairs(act, body)
        it = NQ * ITERS - 1
        gru_r(1, it)
        gru_nz(1, it)
        read_u(NQ, 1, "tp0")
        read_u(NQ, 1, "tp1")

    @blk.vector
    def _(dve):
        dve.wait_ge(loaded, 16 * 9)
        dve.tensor_tensor(bias[:, 0:2], bih[:, 0:2], bhh[:, 0:2], ALU.add).then_inc(prep_v, 1)
        dve.wait_ge(prep_v, 1)
        dve.tensor_scalar_mul(bias[:, 0:2], bias[:, 0:2], 0.5).then_inc(prep_v, 1)
        dve.tensor_scalar_mul(bias[:, 2:3], bhh[:, 2:3], 0.5).then_inc(prep_v, 1)
        dve.tensor_scalar_mul(w_slot[:], w_slot[:], SCALE).then_inc(prep_v, 1)

        def mean_ctx(q, k):
            dve.wait_ge(ctx_sumsq[k], q * GB + GB)
            dve.tensor_scalar(ctx_ss[:, k], ctx_ss[:, k], 1.0 / P, RMS_EPS, ALU.mult, ALU.add).then_inc(ctx_ms[k], 1)

        def mean_sq(lane, it):
            dve.wait_ge(pe1[lane], ev(PE1, "ssq", it))
            dve.tensor_scalar(ms[lane][:], ps_s[lane][:, 0:T:P], 1.0 / P, RMS_EPS, ALU.mult, ALU.add).then_inc(dve1[lane], 1)

        def slots_normed(lane, it, par):
            dve.wait_ge(pe1[lane], ev(PE1, "rbc", it))
            dve.tensor_tensor(sn[lane][:], h[par][lane][:], ps_s[lane][:], ALU.mult).then_inc(dve1[lane], 1)

        def maxima(lane, it):
            dve.wait_ge(pe1[lane], ev(PE1, "scores", it))
            dve.reduce_max(mx[lane][:], ps_s[lane][0:M].rearrange("m (b s) -> m b s", b=GB), AX_X).then_inc(dve1[lane], 1)
            dve.wait_ge(dve1[lane], ev(V, "mx", it))
            dve.tensor_scalar_mul(nmx[lane][:], mx[lane][:], -1.0).then_inc(dve1[lane], 1)

        def normaliser(lane, it):
            dve.wait_ge(exped[lane], it * GB + GB)
            dve.reciprocal(rse[lane][:], se[lane][:]).then_inc(dve1[lane], 1)

        def denominators(lane, it):
            dve.wait_ge(pe1[lane], ev(PE1, "den", it))
            dve.tensor_scalar_add(dn[lane][:], ps_s[lane][:, 0:T:P], RMS_EPS).then_inc(dve1[lane], 1)
            dve.wait_ge(dve1[lane], ev(V, "dn", it))
            dve.reciprocal(rdn[lane][:], dn[lane][:]).then_inc(dve1[lane], 1)

        def weights(lane, it):
            dve.wait_ge(pe1[lane], ev(PE1, "dbc", it))
            for b in range(GB):
                s = slice(b * P, (b + 1) * P)
                ins = dve.scalar_tensor_tensor(at[lane][:, s], ex[lane][:, s], rse[lane][:, b:b + 1], ps_s[lane][0:M, s], ALU.mult, ALU.mult)
            ins.then_inc(dve1[lane], 1)

        def gate_n(lane, it):
            dve.wait_ge(act2[lane], ev(A2, "tr", it))
            dve.scalar_tensor_tensor(rh[:], tr[:], 1.0, hnb[:], ALU.add, ALU.mult).then_inc(dve2[lane], 1)
            dve.wait_ge(dve2[lane], ev(V2, "rh", it))
            dve.wait_ge(pe2[lane], ev(PE2, "xn", it))
            dve.tensor_tensor(pre[:], rh[:], ps_xn[:], ALU.add).then_inc(dve2[lane], 1)

        def update(lane, it, par):
            dve.wait_ge(act2[lane], ev(A2, "nn", it))
            dve.tensor_tensor(df[:], h[par][lane][:], nn[:], ALU.subtract).then_inc(dve2[lane], 1)
            dve.wait_ge(act2[lane], ev(A2, "tz", it))
            dve.wait_ge(dve2[lane], ev(V2, "df", it))
            dve.scalar_tensor_tensor(zd[:], tz[:], 1.0, df[:], ALU.add, ALU.mult).then_inc(dve2[lane], 1)

        def new_h(lane, it, par):
            dve.wait_ge(dve2[lane], ev(V2, "zd", it))
            dve.scalar_tensor_tensor(h[par][lane][:], zd[:], 0.5, nn[:], ALU.mult, ALU.add).then_inc(dve2[lane], 1)

        def residual(lane, q, par):
            dve.wait_ge(dve2[lane], ev(V2, "h", q * ITERS + ITERS - 1))
            g = q * 2 + lane
            need(dve, u_read, u_read_tp(lane, q - 1))
            dve.tensor_tensor(res2[lane][:], h[par][lane][:], x1T[:, bass.ds(g * T, T)], ALU.add).then_inc(post_v[lane], 1)

        def statistics(lane, q):
            dve.wait_ge(u_read, u_value(q + 1, f"tp{lane}"))
            for b in range(GB):
                ins = dve.bn_stats(stats2[lane][:, b], tok[lane][:, b])
            ins.then_inc(post_v[lane], 1)
            hold(dve, post_v[lane], ev(POSTV, "stats", q), passed2[0])
            for b in range(GB):
                ins = dve.bn_aggr(mv2[lane][:, b], stats2[lane][:, b])
            ins.then_inc(post_v[lane], 1)
            dve.wait_ge(post_v[lane], ev(POSTV, "aggr", q))
            dve.tensor_scalar_add(veps2[lane][:], mv2[lane][:, :, 1], LN_EPS).then_inc(post_v[lane], 1)

        def normed(lane, q):
            dve.wait_ge(post_root[lane], q + 1)
            g = q * 2 + lane
            for b in range(GB):
                ins = dve.tensor_scalar(x2[:, bass.ds(g * GB + b, 1), :].rearrange("p o d -> p (o d)"), tok[lane][:, b],
                                        mv2[lane][:, b, 0:1], rstd2[lane][:, b:b + 1], ALU.subtract, ALU.mult)
            ins.then_inc(post_v[lane], 1)

        mean_ctx(0, 0)
        mean_ctx(0, 1)
        mean_ctx(1, 0)

        def body(i, par, first, last):
            for beat, (a, it, j, q, _), (b, it2, j2, q2, par2) in beats(i, par):
                working = not (first and beat == 0)
                mean_sq(a, it)
                if beat in (0, 1) and not first:
                    residual(beat, i - 1, 1 - par)
                if working:
                    gate_n(b, it2)
                slots_normed(a, it, par)
                if working:
                    update(b, it2, par2)
                maxima(a, it)
                if working:
                    new_h(b, it2, par2)
                if beat in (1, 2) and not first:
                    statistics(beat - 1, i - 1)
                normaliser(a, it)
                denominators(a, it)
                weights(a, it)
                if beat in (2, 3) and not first:
                    normed(beat - 2, i - 1)
                if beat == 2 and not last:
                    mean_ctx(i + 1, 1)
                if beat == 5 and not last and not (isinstance(i, int) and i == NQ - 2):
                    mean_ctx(i + 2, 0)
        over_pairs(dve, body)
        it = NQ * ITERS - 1
        gate_n(1, it)
        update(1, it, 1)
        new_h(1, it, 1)
        for lane in range(2):
            residual(lane, NQ - 1, 1)
        for lane in range(2):
            statistics(lane, NQ - 1)
            normed(lane, NQ - 1)

    @blk.tensor
    def _(pe):
        pe.wait_ge(loaded, 16 * 9)
        for j, w in enumerate((wih, whh)):
            for k in range(3):
                ins = pe.transpose(ps_u[j][:, k * P:(k + 1) * P], w[:, k], ident[:])
            ins.then_inc(prep_pe, 1)
        pe.wait_ge(prep_act, 1)
        pe.matmul(ps_u[0][:, 0:P], wk[:], wq[:], start=True, stop=True).then_inc(prep_pe, 1)
        pe.wait_ge(prep_act, 2)
        pe.matmul(ps_u[1][:, 0:3 * P], wv[:], wihT[:], start=True, stop=True).then_inc(prep_pe, 1)
        pe.wait_ge(prep_act, 4)
        pe.wait_ge(const2, 2)

        def make_u(i, par, name):
            value = u_value(i, name)
            need(pe, u_read, value - 1)
            if name[0] == "P":
                k = int(name[1])
                pe.wait_ge(ctx_normed[k], i + 2)
                for b in range(GB):
                    ins = pe.transpose(ps_u[0][:, b * M:(b + 1) * M], pn[:, k, b], ident[0:M, 0:M])
            elif name[0] == "K":
                ins = pe.matmul(ps_u[1][:, 0:GB * M], kq_w[:], pnT[:], start=True, stop=True)
            elif name[0] == "v":
                b = int(name[2])
                ins = pe.matmul(ps_u[b % 2][0:M, 0:3 * P], pnT[:, b * M:(b + 1) * M], vw_w[:], start=True, stop=True)
            else:
                lane = int(name[2])
                pe.wait_ge(post_v[lane], ev(POSTV, "res2", i - 1))
                for b in range(GB):
                    ins = pe.transpose(ps_u[1][:, b * P:(b + 1) * P], res2[lane][:, b * P:(b + 1) * P], ident[:])
            ins.then_inc(u_full, 1)

        def ssq(lane, it):
            pe.wait_ge(squared[lane], it + 1)
            need(pe, dve1[lane], ev(V, "attn", it - 1))
            for b in range(GB):
                ins = pe.matmul(ps_s[lane][:, b * P:(b + 1) * P], sq[lane][:, b * P:(b + 1) * P], ones[:], start=True, stop=True)
            ins.then_inc(pe1[lane], 1)

        def root_spread(lane, it):
            pe.wait_ge(rooted[lane], it + 1)
            for b in range(GB):
                ins = pe.matmul(ps_s[lane][:, b * P:(b + 1) * P], rs[lane][:, b:b + 1].broadcast_to([P, P]), ident[:], start=True, stop=True)
            ins.then_inc(pe1[lane], 1)

        def scores(lane, it, par):
            pe.wait_ge(dve1[lane], ev(V, "sn", it))
            for b in range(GB):
                ins = pe.matmul(ps_s[lane][0:M, b * P:(b + 1) * P], kq[:, par, lane, b * M:(b + 1) * M], sn[lane][:, b * P:(b + 1) * P], start=True, stop=True)
            ins.then_inc(pe1[lane], 1)

        def den(lane, it):
            pe.wait_ge(dve1[lane], ev(V, "rse", it))
            for b in range(GB):
                ins = pe.matmul(ps_s[lane][:, b * P:(b + 1) * P], ex[lane][:, b * P:(b + 1) * P], rse[lane][:, b:b + 1].broadcast_to([M, P]), start=True, stop=True)
            ins.then_inc(pe1[lane], 1)

        def den_spread(lane, it):
            pe.wait_ge(dve1[lane], ev(V, "rdn", it))
            for b in range(GB):
                ins = pe.matmul(ps_s[lane][0:M, b * P:(b + 1) * P], rdn[lane][:, b:b + 1].broadcast_to([P, M]), ident[:], start=True, stop=True)
            ins.then_inc(pe1[lane], 1)

        def gates_h(lane, it, j, q, par):
            other, oit = 1 - lane, it if lane == 1 else it - 1
            if j == 0:
                pe.wait_ge(h_loaded[lane], q + 1)
            need(pe, act2[other], ev(A2, "tz", oit))
            pe.matmul(ps_hn[:], whhT[:, 2 * P:], h[par][lane][:], start=True, stop=True).then_inc(pe2[lane], 1)
            pe.matmul(ps_r[:], whhT[:, 0:P], h[par][lane][:], start=True, stop=False, skip_group_check=True)
            pe.matmul(ps_z[:], whhT[:, P:2 * P], h[par][lane][:], start=True, stop=False, skip_group_check=True)

        def gate_x(lane, it, par, name):
            k, bank = {"r": (0, ps_r), "z": (1, ps_z), "xn": (2, ps_xn)}[name]
            pe.wait_ge(dve1[lane], ev(V, "attn", it))
            if name == "xn":
                need(pe, dve2[1 - lane], ev(V2, "pre", it if lane == 1 else it - 1))
            for b in range(GB):
                ins = pe.matmul(bank[:, b * P:(b + 1) * P], vw[:, par, lane, b, k * P:(k + 1) * P], at[lane][:, b * P:(b + 1) * P],
                                start=name == "xn", stop=name == "xn" or b == GB - 1, skip_group_check=True)
            ins.then_inc(pe2[lane], 1)

        for name in CONTEXT:
            make_u(-1, 1, name)
        pe.wait_ge(u_read, len(CONTEXT))

        def body(i, par, first, last):
            for beat, (a, it, j, q, _), (b, it2, j2, q2, par2) in beats(i, par):
                working = not (first and beat == 0)
                if beat == 0 and not first:
                    pe.wait_ge(u_read, u_value(i - 1, "v13"))
                ssq(a, it)
                if working:
                    gate_x(b, it2, par2, "r")
                    gate_x(b, it2, par2, "xn")
                root_spread(a, it)
                if working:
                    gate_x(b, it2, par2, "z")
                scores(a, it, par)
                for name in u_names(beat, 0, first, last):
                    make_u(i, par, name)
                gates_h(a, it, j, q, par)
                for name in u_names(beat, 1, first, last):
                    make_u(i, par, name)
                den(a, it)
                den_spread(a, it)
        over_pairs(pe, body)
        it = NQ * ITERS - 1
        gate_x(1, it, 1, "r")
        gate_x(1, it, 1, "xn")
        gate_x(1, it, 1, "z")
        make_u(NQ, 1, "tp0")
        make_u(NQ, 1, "tp1")

    block.__exit__(None, None, None)


ROWS = 256


def expert_stage(nc, t, sb, psum, sem, x2, ident, out):
    B = x2.shape[1]
    NE = t["L0_ffn_Wr"].shape[1]
    FF = t["L0_ffn_W1"].shape[2]
    FC = FF // P
    NG = B // GB
    NJ = (B * P + NE * (ROWS - 1)) // ROWS
    HALVES = ROWS // P
    NBUF = 4
    PEEL = NBUF + 3
    assert NBUF % 2 == 0 and (NJ - PEEL) % NBUF == 0 and FC == 4 and B * NE == 512
    xs = nc.dram_tensor("sorted_x", [NJ * ROWS, P], F32).ap()
    ys = nc.dram_tensor("sorted_y", [NJ * ROWS, P], F32).ap()
    w_r = sb("w_r", [P, NE])
    b_r = sb("b_r", [P, NE])
    zero = sb("zero", [P, P])
    all_ones = sb("all_ones", [P, P])
    before = sb("before", [P, P])
    e_index = sb("e_index", [P, NE])
    j_index = sb("j_index", [P, NJ])
    m_half3 = sb("m_half3", [P, GB])
    carry = sb("carry", [P, NE, B])
    x2T = sb("x2T", [P, 2, T])
    x_stage = sb("x_stage", [P, 2, GB, P])
    route = sb("route", [P, B, NE])
    gate = sb("gate", [P, B])
    cand = sb("cand", [P, B, NE])
    which = sb("which", [P, B])
    one_hot = sb("one_hot", [P, NE, B])
    totals = sb("totals", [P, NE, B])
    upto = sb("upto", [P, NE, B])
    place = sb("place", [P, NE, B])
    count_i = sb("count_i", [P, NE], I32)
    tiles = sb("tiles", [P, NE])
    tiles_end = sb("tiles_end", [P, NE])
    start = sb("start", [P, NE])
    dest_f = sb("dest_f", [P, B])
    dest = sb("dest", [P, B], I32)
    ended = sb("ended", [P, NJ, NE])
    tile_e = sb("tile_e", [P, NJ])
    expert = sb("expert", [P, NJ], I32)
    w1 = sb("w1", [P, NBUF, FF])
    w2 = sb("w2", [P, NBUF, FC, P])
    xrow = sb("xrow", [P, NBUF, HALVES, P])
    xcol = sb("xcol", [P, 2, ROWS])
    act_h = sb("act_h", [P, 2, FC, ROWS])
    yrow = sb("yrow", [P, NBUF, HALVES, P])
    yg = sb("yg", [P, B, P])
    stats3 = sb("stats3", [P, 2, GB, 6])
    mv3 = sb("mv3", [P, 2, GB, 2])
    veps3 = sb("veps3", [P, 2, GB])
    rstd3 = sb("rstd3", [P, 2, GB])
    fin = sb("fin", [P, 2, GB, P])
    ps_t = [psum(f"ps_t{k}", [P, T]) for k in range(2)]
    ps_h = [[psum(f"ps_h{k}{m}", [P, T]) for m in range(2)] for k in range(2)]
    ps_l = psum("ps_l", [P, T])
    ps_yy = psum("ps_yy", [P, T])

    loaded3 = sem("loaded3")
    const3 = sem("const3")
    const_v = sem("const_v")
    cleared = sem("cleared")
    staged = sem("staged")
    t_full = sem("t_full")
    t_read = sem("t_read")
    logits_done = sem("logits_done")
    summed = sem("summed")
    sigmoids = sem("sigmoids")
    step = sem("step")
    scattered = sem("scattered")
    tile_in = [sem(f"tile_in{k}") for k in range(NBUF)]
    xcol_full = sem("xcol_full")
    xcol_read = sem("xcol_read")
    h_full = sem("h_full")
    h_act = sem("h_act")
    y_full = sem("y_full")
    y_read = sem("y_read")
    y_stored = [sem(f"y_stored{k}") for k in range(NBUF)]
    gathered = [sem(f"gathered{k}") for k in range(2)]
    fin_step = sem("fin_step")
    fin_root = sem("fin_root")
    fin_done = sem("fin_done")
    stored = [sem(f"stored{k}") for k in range(2)]
    passed3 = sem("passed3")
    N_STEPS = 17

    block = nc.Block()
    blk = block.__enter__()

    def over_tiles(eng, tile):
        for j in range(PEEL):
            tile(j, j % NBUF, j // NBUF)
        with eng.Fori(0, (NJ - PEEL) // NBUF) as i:
            for k in range(NBUF):
                j = PEEL + k
                tile(i * NBUF + j, j % NBUF, i + j // NBUF)

    ov = out.rearrange("(g b) l d -> l g b d", b=GB)

    @blk.sync
    def _(sp):
        sp.dma_start(w_r[:], t["L0_ffn_Wr"]).then_inc(loaded3, 16)
        sp.dma_start(b_r[:], t["L0_ffn_br"].rearrange("(o e) -> o e", o=1).broadcast_to([P, NE])).then_inc(loaded3, 16)
        sp.wait_ge(const3, 1)
        sp.dma_start(xs.rearrange("(k p) d -> p k d", p=P),
                     zero[:].rearrange("p (o d) -> p o d", o=1).broadcast_to([P, NJ * HALVES, P])).then_inc(cleared, 16)
        sp.wait_ge(step, N_STEPS)

        def weights(j, buf):
            e = sp.value_load(expert[0:1, bass.ds(j, 1)], min_val=0, max_val=NE - 1)
            sp.dma_start(w1[:, buf], t["L0_ffn_W1"][bass.ds(e, 1)].rearrange("e d f -> d (e f)")).then_inc(tile_in[buf], 16)
            sp.dma_start(w2[:, buf], t["L0_ffn_W2"][bass.ds(e, 1)].rearrange("e (c p) d -> p (e c) d", p=P)).then_inc(tile_in[buf], 16)

        def tile(j, buf, turn):
            need(sp, y_full, j - (NBUF - 1))
            sp.dma_start(xrow[:, buf], xs[bass.ds(j * ROWS, ROWS)].rearrange("(s p) d -> p s d", p=P)).then_inc(tile_in[buf], 16)
            if not isinstance(j, int) or j >= NBUF:
                weights(j, buf)
        for j in range(NBUF):
            weights(j, j)
        sp.wait_ge(scattered, 16 * B)
        over_tiles(sp, tile)
        with sp.Fori(0, NG // 2) as i:
            for par in range(2):
                g = i * 2 + par
                sp.wait_ge(fin_done, g + 1)
                sp.dma_start(ov[:, bass.ds(g, 1)].rearrange("l g b d -> l (g b) d"), fin[:, par]).then_inc(stored[par], 16)
        for par in range(2):
            sp.wait_ge(stored[par], 16 * NG // 2)

    @blk.gpsimd
    def _(pool):
        pool.memset(zero[:], 0.0).then_inc(const3, 1)
        pool.memset(all_ones[:], 1.0).then_inc(const3, 1)
        pool.memset(m_half3[:], -0.5).then_inc(const3, 1)
        pool.memset(carry[:], 1.0).then_inc(const3, 1)
        pool.iota(e_index[:], pattern=[[1, NE]], base=0, channel_multiplier=0, allow_small_or_imprecise_dtypes=True).then_inc(const3, 1)
        pool.iota(j_index[:], pattern=[[1, NJ]], base=0, channel_multiplier=0, allow_small_or_imprecise_dtypes=True).then_inc(const3, 1)
        pool.wait_ge(const3, 6)
        pool.memset(carry[:, :, 0:1], 0.0).then_inc(const3, 1)
        pool.affine_select(out=before[:], in_=all_ones[:], compare_op=ALU.is_gt, fill=0.0, base=0,
                           pattern=[[1, P]], channel_multiplier=-1).then_inc(const3, 1)
        pool.wait_ge(cleared, 16)
        pool.wait_ge(step, N_STEPS)
        for b in range(B):
            pool.indirect_dma_start(xs, bass.IndirectOffsetOnAxis(ap=dest[:, b:b + 1], axis=0), x2[:, b, :], None).then_inc(scattered, 16)
        for buf in range(NBUF):
            pool.wait_ge(y_stored[buf], 16 * len(range(buf, NJ, NBUF)))
        for g in range(NG):
            par = g % 2
            if g >= 2:
                pool.wait_ge(gathered[par], 16 * GB * (g // 2))
            for b in range(g * GB, (g + 1) * GB):
                pool.indirect_dma_start(yg[:, b, :], None, ys, bass.IndirectOffsetOnAxis(ap=dest[:, b:b + 1], axis=0)).then_inc(gathered[par], 16)
            if g >= 2:
                pool.wait_ge(fin_step, 4 * (g - 2) + 4)
                pool.tensor_tensor(rstd3[:, par], veps3[:, par], m_half3[:], ALU.pow).then_inc(fin_root, 1)
        for g in range(NG, NG + 2):
            pool.wait_ge(fin_step, 4 * (g - 2) + 4)
            pool.tensor_tensor(rstd3[:, g % 2], veps3[:, g % 2], m_half3[:], ALU.pow).then_inc(fin_root, 1)

    @blk.scalar
    def _(act):
        with act.Fori(0, NG // 2) as i:
            for par in range(2):
                g = i * 2 + par
                act.wait_ge(t_full, g + 1)
                act.copy(x2T[:, par], ps_t[par][:]).then_inc(t_read, 1)
        act.wait_ge(step, 1)
        act.activation(route[:], route[:], ACT.Sigmoid).then_inc(sigmoids, 1)

        def store(j, buf):
            act.wait_ge(y_read, j + 1)
            act.dma_start(ys[bass.ds(j * ROWS, ROWS)].rearrange("(s p) d -> p s d", p=P), yrow[:, buf]).then_inc(y_stored[buf], 16)

        def tile(j, buf, turn):
            par = buf % 2
            for m in range(2):
                act.wait_ge(h_full, j * 2 + m + 1)
                if m == 0:
                    need(act, y_full, j - 1)
                act.activation(act_h[:, par, 2 * m:2 * m + 2].rearrange("p c r -> p (c r)"), ps_h[par][m][:], ACT.Gelu).then_inc(h_act, 1)
            if not isinstance(j, int) or j >= 2:
                store(j - 2, (buf - 2) % NBUF)
        over_tiles(act, tile)
        store(NJ - 2, (NJ - 2) % NBUF)
        store(NJ - 1, (NJ - 1) % NBUF)

    @blk.vector
    def _(dve):
        done = [0]

        def link(ins):
            done[0] += 1
            ins.then_inc(step, 1)
            dve.wait_ge(step, done[0])

        def over_b(ap, n):
            return ap.rearrange("p (o e) -> p o e", o=1).broadcast_to([P, n, NE])

        def over_e(ap):
            return ap.rearrange("p (b o) -> p b o", o=1).broadcast_to([P, B, NE])

        def stage_group(g, par, first):
            if not first:
                dve.wait_ge(t_full, g - 1)
            dve.tensor_copy(x_stage[:, par], x2[:, bass.ds(g * GB, GB)]).then_inc(staged, 1)
        stage_group(0, 0, True)
        stage_group(1, 1, True)
        with dve.Fori(1, NG // 2) as i:
            stage_group(i * 2, 0, False)
            stage_group(i * 2 + 1, 1, False)
        dve.wait_ge(loaded3, 32)
        dve.wait_ge(const3, 8)
        dve.wait_ge(logits_done, NG)
        link(dve.tensor_tensor(route[:], ps_l[:].rearrange("p (b e) -> p b e", e=NE), over_b(b_r[:], B), ALU.add))
        dve.wait_ge(sigmoids, 1)
        link(dve.reduce_max(gate[:], route[:], AX_X))
        link(dve.tensor_tensor(cand[:], route[:], over_e(gate[:]), ALU.is_lt))
        link(dve.scalar_tensor_tensor(cand[:], cand[:], float(NE), over_b(e_index[:], B), ALU.mult, ALU.add))
        link(dve.tensor_reduce(which[:], cand[:], AX_X, ALU.min))
        link(dve.tensor_tensor(one_hot[:].rearrange("p e b -> p b e"), over_b(e_index[:], B), over_e(which[:]), ALU.is_equal))
        dve.wait_ge(summed, 2)
        flat = "p e b -> p (e b)"
        link(dve.tensor_copy(totals[:].rearrange(flat), ps_t[1][:]))
        link(dve.tensor_tensor_scan(upto[:].rearrange(flat), carry[:].rearrange(flat), totals[:].rearrange(flat), 0.0, ALU.mult, ALU.add))
        link(dve.tensor_scalar_add(count_i[:], upto[:, :, B - 1], float(ROWS - 1)))
        link(dve.tensor_single_scalar(count_i[:], count_i[:], ROWS.bit_length() - 1, ALU.logical_shift_right))
        link(dve.tensor_copy(tiles[:], count_i[:]))
        link(dve.tensor_tensor_scan(tiles_end[:], all_ones[:, 0:NE], tiles[:], 0.0, ALU.mult, ALU.add))
        dve.tensor_tensor(start[:], tiles_end[:], tiles[:], ALU.subtract).then_inc(const_v, 1)
        dve.tensor_tensor(upto[:], upto[:], totals[:], ALU.subtract).then_inc(const_v, 1)
        dve.tensor_tensor(ended[:], over_b(tiles_end[:], NJ), j_index[:].rearrange("p (j o) -> p j o", o=1).broadcast_to([P, NJ, NE]), ALU.is_le).then_inc(const_v, 1)
        dve.wait_ge(const_v, 3)
        dve.tensor_reduce(tile_e[:], ended[:], AX_X, ALU.add).then_inc(const_v, 1)
        dve.tensor_tensor(place[:].rearrange(flat), upto[:].rearrange(flat), ps_t[0][:], ALU.add).then_inc(const_v, 1)
        dve.wait_ge(const_v, 5)
        dve.tensor_scalar(expert[:], tile_e[:], float(NE - 1), None, ALU.min).then_inc(const_v, 1)
        link(dve.scalar_tensor_tensor(place[:], start[:].rearrange("p (e o) -> p e o", o=1).broadcast_to([P, NE, B]), float(ROWS), place[:], ALU.mult, ALU.add))
        link(dve.tensor_tensor(place[:], place[:], one_hot[:], ALU.mult))
        link(dve.tensor_reduce(dest_f[:], place[:].rearrange("p e b -> p b e"), AX_X, ALU.add))
        dve.wait_ge(const_v, 6)
        link(dve.tensor_copy(dest[:], dest_f[:]))
        link(dve.memset(stats3[:], 0.0))
        assert done[0] == N_STEPS

        def store_y(j, buf, turn):
            dve.wait_ge(y_full, j + 1)
            need(dve, y_stored[buf], turn * 16)
            dve.tensor_copy(yrow[:, buf].rearrange("p s d -> p (s d)"), ps_yy[:, 0:ROWS]).then_inc(y_read, 1)

        def tile(j, buf, turn):
            dve.wait_ge(xcol_full, j + 1)
            need(dve, h_full, 2 * j - 2)
            dve.tensor_copy(xcol[:, buf % 2], ps_t[buf % 2][:, 0:ROWS]).then_inc(xcol_read, 1)
            if not isinstance(j, int) or j >= 2:
                last = (buf - 2) % NBUF
                store_y(j - 2, last, turn if buf >= 2 else turn - 1)
        over_tiles(dve, tile)
        for j in range(NJ - 2, NJ):
            store_y(j, j % NBUF, j // NBUF)

        def finish_pair(i, first):
            for par in range(2):
                g = i * 2 + par
                dve.wait_ge(gathered[par], i * (16 * GB) + 16 * GB)
                for b in range(GB):
                    s = g * GB + b
                    ins = dve.scalar_tensor_tensor(yg[:, bass.ds(s, 1)].rearrange("p o d -> p (o d)"), yg[:, bass.ds(s, 1)].rearrange("p o d -> p (o d)"),
                                                   gate[:, bass.ds(s, 1)], x2[:, bass.ds(s, 1)].rearrange("p o d -> p (o d)"), ALU.mult, ALU.add)
                ins.then_inc(fin_step, 1)
                hold(dve, fin_step, g * 4 + 1, passed3)
                for b in range(GB):
                    ins = dve.bn_stats(stats3[:, par, b], yg[:, bass.ds(g * GB + b, 1)].rearrange("p o d -> p (o d)"))
                ins.then_inc(fin_step, 1)
                hold(dve, fin_step, g * 4 + 2, passed3)
                for b in range(GB):
                    ins = dve.bn_aggr(mv3[:, par, b], stats3[:, par, b])
                ins.then_inc(fin_step, 1)
                dve.wait_ge(fin_step, g * 4 + 3)
                dve.tensor_scalar_add(veps3[:, par], mv3[:, par, :, 1], LN_EPS).then_inc(fin_step, 1)
                dve.wait_ge(fin_root, g + 1)
                if not first:
                    dve.wait_ge(stored[par], i * 16)
                for b in range(GB):
                    ins = dve.tensor_scalar(fin[:, par, b], yg[:, bass.ds(g * GB + b, 1)].rearrange("p o d -> p (o d)"),
                                            mv3[:, par, b, 0:1], rstd3[:, par, b:b + 1], ALU.subtract, ALU.mult)
                ins.then_inc(fin_done, 1)

        finish_pair(0, True)
        with dve.Fori(1, NG // 2) as i:
            finish_pair(i, False)

    @blk.tensor
    def _(pe):
        pe.wait_ge(loaded3, 32)
        def group(g, par, first):
            if not first:
                pe.wait_ge(t_read, g - 1)
            pe.wait_ge(staged, g + 1)
            for b in range(GB):
                ins = pe.transpose(ps_t[par][:, b * P:(b + 1) * P], x_stage[:, par, b], ident[:])
            ins.then_inc(t_full, 1)
            pe.wait_ge(t_read, g + 1)
            for b in range(GB):
                ins = pe.matmul(ps_l[:, bass.ds(g * (GB * NE) + b * NE, NE)], x2T[:, par, b * P:(b + 1) * P], w_r[:], start=True, stop=True)
            ins.then_inc(logits_done, 1)
        group(0, 0, True)
        group(1, 1, True)
        with pe.Fori(1, NG // 2) as i:
            group(i * 2, 0, False)
            group(i * 2 + 1, 1, False)
        pe.wait_ge(const3, 8)
        pe.wait_ge(step, 6)
        hot = one_hot[:].rearrange("p e b -> p (e b)")
        pe.matmul(ps_t[0][:], before[:], hot, start=True, stop=True).then_inc(summed, 1)
        pe.matmul(ps_t[1][:], all_ones[:], hot, start=True, stop=True).then_inc(summed, 1)
        pe.wait_ge(step, N_STEPS)

        def transposed(j, buf, turn):
            par = buf % 2
            pe.wait_ge(tile_in[buf], turn * 48 + 48)
            need(pe, xcol_read, j - 1)
            for s in range(HALVES):
                ins = pe.transpose(ps_t[par][:, s * P:(s + 1) * P], xrow[:, buf, s], ident[:])
            ins.then_inc(xcol_full, 1)

        def up(j, buf):
            par = buf % 2
            pe.wait_ge(xcol_read, j + 1)
            for m in range(2):
                need(pe, h_act, j * 2 - 4 + m + 1)
                for k in range(2):
                    c = 2 * m + k
                    ins = pe.matmul(ps_h[par][m][:, k * ROWS:(k + 1) * ROWS], w1[:, buf, c * P:(c + 1) * P], xcol[:, par], start=True, stop=True)
                ins.then_inc(h_full, 1)

        def down(j, buf):
            par = buf % 2
            pe.wait_ge(h_act, j * 2 + 2)
            need(pe, y_read, j)
            for s in range(HALVES):
                for c in range(FC):
                    ins = pe.matmul(ps_yy[:, s * P:(s + 1) * P], act_h[:, par, c, s * P:(s + 1) * P], w2[:, buf, c], start=c == 0, stop=c == FC - 1)
            ins.then_inc(y_full, 1)

        def tile(j, buf, turn):
            transposed(j, buf, turn)
            if not isinstance(j, int) or j >= 1:
                up(j - 1, (buf - 1) % NBUF)
            if not isinstance(j, int) or j >= 2:
                down(j - 2, (buf - 2) % NBUF)
        over_tiles(pe, tile)
        up(NJ - 1, (NJ - 1) % NBUF)
        down(NJ - 2, (NJ - 2) % NBUF)
        down(NJ - 1, (NJ - 1) % NBUF)

    block.__exit__(None, None, None)


_INS = ['x', 'ctx_1024', 'L0_attn_W_in', 'L0_attn_conv_w', 'L0_attn_conv_b', 'L0_attn_W_x', 'L0_attn_W_dt',
        'L0_attn_b_dt', 'L0_attn_A_log', 'L0_attn_D', 'L0_attn_W_out', 'L0_xattn_Wq', 'L0_xattn_Wk',
        'L0_xattn_Wv', 'L0_xattn_gru_wih', 'L0_xattn_gru_whh', 'L0_xattn_gru_bih', 'L0_xattn_gru_bhh',
        'L0_xattn_slot_norm_w', 'L0_xattn_input_norm_w', 'L0_ffn_Wr', 'L0_ffn_br', 'L0_ffn_W1', 'L0_ffn_W2']


def kernel(**inputs):
    import numpy as np
    import concourse.bacc as bacc
    from concourse import mybir as mb
    from concourse.bass_utils import run_bass_kernel_spmd as run

    nc = bacc.Bacc("TRN2", target_bir_lowering=False, num_devices=1)
    arrays, tensors = {}, {}
    for name in _INS:
        a = np.ascontiguousarray(inputs[name])
        arrays[f"in_{name}"] = a
        tensors[name] = nc.dram_tensor(f"in_{name}", a.shape, mb.dt.from_np(a.dtype), kind="ExternalInput").ap()
    out = nc.dram_tensor("out_x", OUT_SHAPE, F32, kind="ExternalOutput").ap()
    build_program(nc, tensors, out)
    r = run(nc, [arrays], core_ids=[0])
    return r.results[0]["out_x"]


OUT_SHAPE = (64, 128, 128)
```
